# Optimizing a Trainium2 kernel written in Bass

```python
import numpy as np
import jax
import jax.numpy as jnp

def _softmax(x, axis=-1):
    return jax.nn.softmax(x, axis=axis)

def _gelu(x):
    return jax.nn.gelu(x, approximate=True)

def _silu(x):
    return jax.nn.silu(x)

def _sigmoid(x):
    return jax.nn.sigmoid(x)

def _layernorm(x, axis=-1, eps=1e-05):
    m = jnp.mean(x, axis=axis, keepdims=True)
    v = jnp.var(x, axis=axis, keepdims=True)
    return (x - m) / jnp.sqrt(v + eps)

def _scatter_add(tgt, idx, src, axis=0):
    return tgt.at[idx].add(src)

def _segment_sum(src, seg, n):
    return jax.ops.segment_sum(src, seg, n)
kernel_name = 'mk_macaron_d1_jaxref_r4_38c966'

def setup_inputs(seed: int=0):
    np.random.seed(seed)
    _w = jnp.asarray

    def _L0_attn_setup():
        import jax, jax.numpy as jnp
        import numpy as np
        NUM_HEADS = 16
        CHUNK = 64
        RMS_EPS = 1.1920928955078125e-07

        def _forward(x, w_in, w_out):
            B, S, D = x.shape
            H, hd, C = (NUM_HEADS, D // NUM_HEADS, CHUNK)
            proj = x @ w_in.T
            q, k, v, a, g = jnp.split(proj, 5, axis=-1)
            rs = lambda t: t.reshape(B, S, H, hd)
            q, k, v, a, g = map(rs, (q, k, v, a, g))
            q = q * jax.lax.rsqrt(jnp.mean(q * q, axis=-1, keepdims=True) + RMS_EPS)
            k = jnp.tanh(k)
            a = jnp.clip(jax.nn.sigmoid(a + 2.0), 0.6, 0.9995)
            u = k * v
            NC = S // C
            a_r = a.reshape(B, NC, C, H, hd).transpose(1, 0, 2, 3, 4)
            u_r = u.reshape(B, NC, C, H, hd).transpose(1, 0, 2, 3, 4)

            def step(state, au):
                a_c, u_c = au
                prefix = jnp.cumprod(a_c, axis=1)
                acc = jnp.cumsum(u_c / jnp.maximum(prefix, 1e-06), axis=1)
                states = prefix * (state[:, None] + acc)
                return (states[:, -1], states)
            state0 = jnp.zeros((B, H, hd), dtype=jnp.float32)
            _, mem = jax.lax.scan(step, state0, (a_r, u_r))
            memory = mem.transpose(1, 0, 2, 3, 4).reshape(B, S, H, hd)
            gate = jax.nn.sigmoid(g)
            y = gate * (q * memory) + (1.0 - gate) * v
            return y.reshape(B, S, D) @ w_out.T
        key = jax.random.key(seed)
        k1, k2, k3 = jax.random.split(key, 3)
        B, S, D = (2, 1024, 512)
        x = jax.random.normal(k1, (B, S, D), dtype=jnp.float32)
        w_in = jax.random.normal(k2, (5 * D, D), dtype=jnp.float32) * 0.02
        w_out = jax.random.normal(k3, (D, D), dtype=jnp.float32) * 0.02
        return {'x': x, 'w_in': w_in, 'w_out': w_out}
    _L0_attn_in = _L0_attn_setup()

    def _L0_ffn_setup():
        import jax, jax.numpy as jnp
        import numpy as np
        B, S, D, E, TOPK, H = (8, 512, 512, 8, 2, 16)
        DH = D // H
        FH = D // H
        ROUTE_LEN = 512
        key = jax.random.key(seed)
        ks = jax.random.split(key, 8)
        s = 0.02
        return {'x': jax.random.normal(ks[0], (B, S, D), jnp.float32), 'switch_w': jax.random.normal(ks[1], (E, D * ROUTE_LEN), jnp.float32) * s, 'switch_b': jnp.zeros((E,), jnp.float32), 'w1': jax.random.normal(ks[2], (E, FH, DH), jnp.float32) * s, 'b1': jnp.zeros((E, FH), jnp.float32), 'w2': jax.random.normal(ks[3], (E, DH, FH), jnp.float32) * s, 'b2': jnp.zeros((E, DH), jnp.float32), 'w3': jax.random.normal(ks[4], (D, D), jnp.float32) * s, 'b3': jnp.zeros((D,), jnp.float32)}
    _L0_ffn_in = _L0_ffn_setup()
    _d = {'L0_attn_x': _L0_attn_in['x'], 'L0_attn_w_in': _L0_attn_in['w_in'], 'L0_attn_w_out': _L0_attn_in['w_out'], 'L0_ffn_switch_w': _L0_ffn_in['switch_w'], 'L0_ffn_switch_b': _L0_ffn_in['switch_b'], 'L0_ffn_w1': _L0_ffn_in['w1'], 'L0_ffn_b1': _L0_ffn_in['b1'], 'L0_ffn_w2': _L0_ffn_in['w2'], 'L0_ffn_b2': _L0_ffn_in['b2'], 'L0_ffn_w3': _L0_ffn_in['w3'], 'L0_ffn_b3': _L0_ffn_in['b3']}
    _x0 = _d['L0_attn_x']
    _d['L0_attn_x'] = jax.random.normal(jax.random.fold_in(jax.random.key(seed), 1), (4, 512, 512), dtype=_x0.dtype)
    del _x0
    return _d

def reference(L0_attn_x, L0_attn_w_in, L0_attn_w_out, L0_ffn_switch_w, L0_ffn_switch_b, L0_ffn_w1, L0_ffn_b1, L0_ffn_w2, L0_ffn_b2, L0_ffn_w3, L0_ffn_b3):

    def _L0_attn_ref(x, w_in, w_out):
        import jax, jax.numpy as jnp
        import numpy as np
        NUM_HEADS = 16
        CHUNK = 64
        RMS_EPS = 1.1920928955078125e-07

        def _forward(x, w_in, w_out):
            B, S, D = x.shape
            H, hd, C = (NUM_HEADS, D // NUM_HEADS, CHUNK)
            proj = x @ w_in.T
            q, k, v, a, g = jnp.split(proj, 5, axis=-1)
            rs = lambda t: t.reshape(B, S, H, hd)
            q, k, v, a, g = map(rs, (q, k, v, a, g))
            q = q * jax.lax.rsqrt(jnp.mean(q * q, axis=-1, keepdims=True) + RMS_EPS)
            k = jnp.tanh(k)
            a = jnp.clip(jax.nn.sigmoid(a + 2.0), 0.6, 0.9995)
            u = k * v
            NC = S // C
            a_r = a.reshape(B, NC, C, H, hd).transpose(1, 0, 2, 3, 4)
            u_r = u.reshape(B, NC, C, H, hd).transpose(1, 0, 2, 3, 4)

            def step(state, au):
                a_c, u_c = au
                prefix = jnp.cumprod(a_c, axis=1)
                acc = jnp.cumsum(u_c / jnp.maximum(prefix, 1e-06), axis=1)
                states = prefix * (state[:, None] + acc)
                return (states[:, -1], states)
            state0 = jnp.zeros((B, H, hd), dtype=jnp.float32)
            _, mem = jax.lax.scan(step, state0, (a_r, u_r))
            memory = mem.transpose(1, 0, 2, 3, 4).reshape(B, S, H, hd)
            gate = jax.nn.sigmoid(g)
            y = gate * (q * memory) + (1.0 - gate) * v
            return y.reshape(B, S, D) @ w_out.T
        return _forward(x, w_in, w_out)

    def _L0_ffn_ref(x, switch_w, switch_b, w1, b1, w2, b2, w3, b3):
        import jax, jax.numpy as jnp
        import numpy as np
        B, S, D, E, TOPK, H = (8, 512, 512, 8, 2, 16)
        DH = D // H
        FH = D // H
        ROUTE_LEN = 512
        b, s, d = x.shape
        x0 = x[:, :ROUTE_LEN].reshape(b, -1)
        logits = x0 @ switch_w.T + switch_b
        probs = jax.nn.softmax(logits, axis=-1)
        gate, top_idx = jax.lax.top_k(probs, TOPK)
        xh = x.reshape(b, s, H, DH).transpose(0, 2, 1, 3)
        w1s, b1s = (w1[top_idx], b1[top_idx])
        w2s, b2s = (w2[top_idx], b2[top_idx])
        h = jnp.einsum('bhsd,bkfd->bkhsf', xh, w1s) + b1s[:, :, None, None, :]
        h = jax.nn.gelu(h, approximate=False)
        o = jnp.einsum('bkhsf,bkdf->bkhsd', h, w2s) + b2s[:, :, None, None, :]
        o = (o * gate[:, :, None, None, None]).sum(axis=1)
        o = o.transpose(0, 2, 1, 3).reshape(b, s, d)
        out = x + o
        return out @ w3.T + b3
    x = L0_attn_x
    x = x + 0.5 * _L0_ffn_ref(_layernorm(x, axis=-1), L0_ffn_switch_w, L0_ffn_switch_b, L0_ffn_w1, L0_ffn_b1, L0_ffn_w2, L0_ffn_b2, L0_ffn_w3, L0_ffn_b3)
    x = x + _L0_attn_ref(_layernorm(x, axis=-1), L0_attn_w_in, L0_attn_w_out)
    x = x + 0.5 * _L0_ffn_ref(_layernorm(x, axis=-1), L0_ffn_switch_w, L0_ffn_switch_b, L0_ffn_w1, L0_ffn_b1, L0_ffn_w2, L0_ffn_b2, L0_ffn_w3, L0_ffn_b3)
    return x

_drawn_inputs = setup_inputs


def setup_inputs(seed=0):
    import zlib

    import numpy as np

    out = dict(_drawn_inputs(seed))
    spreads = {'L0_ffn_switch_b': (0.0, 0.1),
     'L0_ffn_b1': (0.0, 0.8),
     'L0_ffn_b2': (0.0, 0.1),
     'L0_ffn_b3': (0.0, 0.1)}
    factors = {'L0_ffn_w1': 8.0, 'L0_ffn_w2': 8.0}
    for name, (base, spread) in spreads.items():
        noise = np.random.default_rng([zlib.crc32(name.encode()), seed]).standard_normal(out[name].shape)
        drawn = base * np.exp(spread * noise) if base else spread * noise
        out[name] = jnp.asarray(drawn.astype(out[name].dtype))
    for name, factor in factors.items():
        out[name] = (out[name] * factor).astype(out[name].dtype)
    return out
```

```python
from contextlib import ExitStack

import concourse.bass as bass
from concourse import mybir

P = 128
ALU = mybir.AluOpType
ACT = mybir.ActivationFunctionType
AX = mybir.AxisListType
F32 = mybir.dt.float32
F32R = mybir.dt.float32r
BF16 = mybir.dt.bfloat16

B, S, D = 4, 512, 512
NT = S // P
KC = D // P
E, TOPK = 8, 2
HD = 32
HPC = P // HD
CHUNK = 64
ROLES = 5
GUARD = 1e-6
LN_EPS = 1e-5
RMS_EPS = 1.1920928955078125e-07
A_MIN, A_MAX = 0.6, 0.9995
FB = HD + 1


JOB_Q, JOB_A, JOB_K, JOB_V, JOB_G = range(ROLES)
IN_JOBS = ROLES * KC
H_JOBS = TOPK * KC


class Steps:

    def __init__(self, eng, sem):
        self.eng, self.sem, self.base, self.n = eng, sem, 0, 0

    def mark(self, ins):
        self.n += 1
        ins.then_inc(self.sem, 1)
        return self.base + self.n

    def wait(self, value):
        self.eng.wait_ge(self.sem, value)

    def do(self, ins):
        self.wait(self.mark(ins))


def macaron_kernel(nc, x, w_in, w_out, switch_w, switch_b, w1, b1, w2, b2, w3, b3, out):
    x2_dram = nc.dram_tensor("x2_dram", (B, S, D), F32).ap()

    with ExitStack() as ctx:
        def sb(name, shape, dt=F32, into=ctx):
            return into.enter_context(nc.sbuf_tensor(name, shape, dt))

        def sem(name):
            return ctx.enter_context(nc.semaphore(name))

        with ExitStack() as region:
            route_w = sb("route_w", [P, NT, E, D], into=region)
        wide = ExitStack()
        win_hi = sb("win_hi", [P, KC, ROLES, KC, P], F32R, into=wide)
        win_lo = sb("win_lo", [P, KC, ROLES, KC, P], BF16, into=wide)
        sb("wide_rest", [P, (NT * E * D - KC * ROLES * KC * P * 3 // 2)], into=wide)
        ctx.enter_context(wide)

        w3_hi = sb("w3_hi", [P, KC, D], F32R)
        w3_lo = sb("w3_lo", [P, KC, D], F32R)
        wo_hi = sb("wo_hi", [P, KC, D], F32R)
        wo_lo = sb("wo_lo", [P, KC, D], F32R)
        xa = sb("xa", [P, NT, D])
        x1 = sb("x1", [P, NT, D])
        xnw = sb("xnw", [P, NT * D])
        with ExitStack() as region:
            xnr = sb("xnr", [P, NT * D], into=region)
        z_lo = sb("z_lo", [P, KC, S], F32R)

        with ExitStack() as region:
            xh = sb("xh", [P, KC, S], F32R, into=region)
            xl = sb("xl", [P, KC, S], F32R, into=region)
            xbf = sb("xbf", [P, KC, S], BF16, into=region)
            q_sq = sb("q_sq", [P, S], into=region)
            rs_hi = sb("rs_hi", [P, NT * HPC, HD], F32R, into=region)
            rs_lo = sb("rs_lo", [P, NT * HPC, HD], F32R, into=region)
            prod = sb("prod", [P, TOPK, FB, E], into=region)
            w_diag = sb("w_diag", [P, TOPK, HPC, HD], into=region)
        xt = sb("xt", [P, KC, S])
        xt_hi = sb("xt_hi", [P, 2, S], F32R)
        xt_lo = sb("xt_lo", [P, 2, S], F32R)
        hf = sb("hf", [P, TOPK, S])
        h_hi = sb("h_hi", [P, TOPK, S], F32R)
        h_lo = sb("h_lo", [P, TOPK, S], F32R)
        z_hi = sb("z_hi", [P, KC, S], F32R)

        with ExitStack() as region:
            raw = sb("raw", [P, 3, ROLES * KC * P], into=region)
        y_hi = sb("y_hi", [P, KC, S], F32R)
        y_lo = sb("y_lo", [P, KC, S], F32R)
        decay = sb("decay", [P, S])
        pref = sb("pref", [P, S])
        kt = sb("kt", [P, S])
        vt = sb("vt", [P, S])
        gt = sb("gt", [P, S])
        qt = sb("qt", [P, S])
        starts = sb("starts", [P, S])

        ident = sb("ident", [P, P])
        ident_r = sb("ident_r", [P, P], F32R)
        ones = sb("ones", [P, P])
        head_of = sb("head_of", [P, HPC])
        diag = sb("diag", [P, HD])
        w1_tab = sb("w1_tab", [P, FB, E])
        w2_tab = sb("w2_tab", [P, FB, E])
        w1_sel = sb("w1_sel", [P, TOPK, FB])
        w2_sel = sb("w2_sel", [P, TOPK, FB])
        b2_col = sb("b2_col", [P, 1])
        w1_hi = sb("w1_hi", [P, TOPK, P], F32R)
        w1_lo = sb("w1_lo", [P, TOPK, P], F32R)
        w2_hi = sb("w2_hi", [P, TOPK, P], F32R)
        w2_lo = sb("w2_lo", [P, TOPK, P], F32R)
        b3_half = sb("b3_half", [P, D])
        sw_bias = sb("sw_bias", [P, E])
        stats = sb("stats", [P, NT, 6])
        mv = sb("mv", [P, B, NT, 2])
        rstd = sb("rstd", [P, B, NT])
        mv1 = sb("mv1", [P, NT, 2])
        rstd1 = sb("rstd1", [P, NT])
        neg_half = sb("neg_half", [P, NT * HPC])
        two = sb("two", [P, 1])
        ms = sb("ms", [P, NT * HPC])
        rs = sb("rs", [P, NT * HPC])
        part = sb("part", [P, E])
        lmix = sb("lmix", [P, B, E])
        lg = sb("lg", [P, B, E])
        eq = sb("eq", [P, B, E])
        rank = sb("rank", [P, E])
        red = sb("red", [P, B])
        fence = sb("fence", [P, 1])
        red2 = sb("red2", [P, B])
        gates = sb("gates", [P, B, TOPK])
        pick = sb("pick", [P, B, TOPK, E])
        pick_g = sb("pick_g", [P, B, TOPK, E])

        banks = [ctx.enter_context(nc.psum_tensor(f"bank{i}", [P, 512], F32)) for i in range(8)]
        in_bank = banks[0:4]
        t_bank = banks[4:6]
        o_bank = banks[6:8]

        s_small = sem("s_small")
        s_xr = [sem(f"s_xr{i}") for i in range(2)]
        s_sw = [sem(f"s_sw{t}") for t in range(NT)]
        s_xa = sem("s_xa")
        s_raw = [sem(f"s_raw{i}") for i in range(6)]
        s_x2 = sem("s_x2")
        s_out = sem("s_out")
        s_pc = sem("s_pc")
        s_vc = sem("s_vc")
        s_whi = sem("s_whi")
        s_wlo = sem("s_wlo")
        s_wlo0 = sem("s_wlo0")
        s_rv = sem("s_rv")
        s_rp = sem("s_rp")
        s_rn = sem("s_rn")
        s_rm = sem("s_rm")
        s_mix = sem("s_mix")
        s_lg = sem("s_lg")
        s_sh = sem("s_sh")
        s_exp = sem("s_exp")
        s_sel = sem("s_sel")
        s_xn = sem("s_xn")
        s_xb = sem("s_xb")
        s_t1 = sem("s_t1")
        s_t1e = sem("s_t1e")
        s_xtl = sem("s_xtl")
        s_h = sem("s_h")
        s_gelu = sem("s_gelu")
        s_hl = sem("s_hl")
        s_ob = sem("s_ob")
        s_obf = sem("s_obf")
        s_zh = sem("s_zh")
        s_zl = sem("s_zl")
        s_v1 = sem("s_v1")
        s_p1 = sem("s_p1")
        s_xn1 = sem("s_xn1")
        s_t2 = sem("s_t2")
        s_t2a = sem("s_t2a")
        s_t2v = sem("s_t2v")
        s_in = sem("s_in")
        s_ina = sem("s_ina")
        s_u = sem("s_u")
        s_sq = sem("s_sq")
        s_rms = sem("s_rms")
        s_ms = sem("s_ms")
        s_rsp = sem("s_rsp")
        s_rsh = sem("s_rsh")
        s_rsl = sem("s_rsl")
        s_rsb = sem("s_rsb")
        s_qn = sem("s_qn")
        s_qm = sem("s_qm")
        s_pd = sem("s_pd")
        s_y = sem("s_y")
        s_yh = sem("s_yh")
        s_yl = sem("s_yl")
        s_xo = sem("s_xo")
        s_fin = sem("s_fin")
        s_ve = sem("s_ve")
        s_po = sem("s_po")
        s_ac = sem("s_ac")

        def ob_expert(f, late):
            return 2 * KC * 0 + (48 + 8 * (f - B) if late else (12 * f - 4 if not isinstance(f, int) or f else 0))

        def ob_w3(f, late):
            return 52 + 8 * (f - B) if late else (12 * f + 4)

        def ob_out(b):
            return (12 * b + 12) if not isinstance(b, int) or b < B - 1 else 12 * b + 8

        def mm3(pe, res, a_hi, a_lo, b_hi, b_lo, start, stop):
            pe.matmul(res, a_hi, b_hi, start=start, stop=False)
            pe.matmul(res, a_hi, b_lo, start=False, stop=False)
            return pe.matmul(res, a_lo, b_hi, start=False, stop=stop)

        block = ctx.enter_context(nc.Block())

        @block.sync
        def _(sp):
            def chunk_of(src, t):
                return src[:, t * P:(t + 1) * P, :].rearrange("b p d -> p b d")

            def row_of(src, f):
                return src[f].rearrange("(t p) d -> p t d", p=P)

            def route_loads(phase, src):
                for t in range(NT):
                    if phase == 1 and t == 0:
                        sp.wait_ge(s_in, IN_JOBS * B)
                        sp.wait_ge(s_x2, 16 * NT * B)
                        sp.wait_ge(s_obf, 44)
                    if t >= 2:
                        sp.wait_ge(s_rn, NT * phase + t - 1)
                    sp.dma_start((xa if t % 2 == 0 else x1)[:], chunk_of(src, t)).then_inc(s_xr[t % 2], 16)
                    sp.dma_start(route_w[:, t], switch_w[:, t]).then_inc(s_sw[t], 16)
                    if phase == 0 and t == 0:
                        sp.dma_start(w1_tab[:, 0:HD, :], w1.partition_broadcast(HPC)).then_inc(s_small, 16)
                        sp.dma_start(w1_tab[:, HD, :], b1.partition_broadcast(HPC)).then_inc(s_small, 16)
                        sp.dma_start(w2_tab[:, 0:HD, :], w2.partition_broadcast(HPC)).then_inc(s_small, 16)
                        sp.dma_start(w2_tab[:, HD, :], b2.partition_broadcast(HPC)).then_inc(s_small, 16)
                        sp.dma_start(b3_half[:], b3.partition_broadcast(P)).then_inc(s_small, 16)
                        sp.dma_start(sw_bias[:], switch_b.partition_broadcast(P)).then_inc(s_small, 16)

            route_loads(0, x)
            sp.wait_ge(s_rn, NT - 1)
            sp.dma_start(xa[:], row_of(x, 0)).then_inc(s_xa, 16)
            sp.dma_start(raw[:, 0, 0:KC * D].rearrange("p (k n) -> p k n", k=KC), w3).then_inc(s_raw[0], 16)
            sp.dma_start(raw[:, 1, 0:KC * D].rearrange("p (k n) -> p k n", k=KC), w_out).then_inc(s_raw[1], 16)
            for g in range(KC):
                if g == 1:
                    sp.wait_ge(s_wlo, 1)
                if g == 2:
                    sp.wait_ge(s_wlo, 2)
                if g == 3:
                    sp.wait_ge(s_wlo0, 1)
                sp.dma_start(raw[:, (g + 2) % 3, :], w_in[g]).then_inc(s_raw[2 + g], 16)

            def body(b, last):
                if not last:
                    sp.wait_ge(s_obf, ob_w3(b, False) + NT)
                    sp.dma_start(xa[:], row_of(x, b + 1)).then_inc(s_xa, 16)
                for t in range(NT):
                    sp.wait_ge(s_xo, NT * b + t + 1)
                    sp.dma_start(x2_dram[b, t * P:(t + 1) * P, :], x1[:, t, :]).then_inc(s_x2, 16)

            with sp.Fori(0, B - 1) as b:
                body(b, False)
            body(B - 1, True)

            route_loads(1, x2_dram)

            def late(f):
                sp.dma_start(xa[:], row_of(x2_dram, f)).then_inc(s_xa, 16)
                for t in range(NT):
                    sp.wait_ge(s_fin, NT * f + t + 1)
                    sp.dma_start(out[f, t * P:(t + 1) * P, :], x1[:, t, :]).then_inc(s_out, 16)

            sp.wait_ge(s_rn, 2 * NT - 1)
            late(0)
            with sp.Fori(1, B) as f:
                late(f)
            sp.wait_ge(s_out, 16 * NT * B)

        @block.tensor
        def _(pe):
            def route(phase):
                if phase == 1:
                    pe.wait_ge(s_obf, 48)
                for t in range(NT):
                    pe.wait_ge(s_sw[t], 16 * (phase + 1))
                    pe.wait_ge(s_rn, NT * phase + t + 1)
                    xn = xnw if t % 2 == 0 else xnr
                    for d in range(D // HD):
                        mm = pe.matmul(o_bank[0][:, 0:E * HD], xn[:, d * P:(d + 1) * P],
                                       route_w[:, t, :, d * HD:(d + 1) * HD],
                                       start=(t == 0 and d == 0), stop=(t == NT - 1 and d == D // HD - 1))
                    mm.then_inc(s_rm, 1)
                if phase == 0:
                    pe.wait_ge(s_vc, 1)
                pe.wait_ge(s_mix, phase + 1)
                pe.matmul(o_bank[1][:, 0:B * E], ones[:], lmix[:].rearrange("p b e -> p (b e)"),
                          start=True, stop=True).then_inc(s_lg, 1)

            def t1(f, first, after_row):
                pe.wait_ge(s_xn, NT * (f + 1))
                for c in range(KC):
                    if c >= 2:
                        pe.wait_ge(s_t1e, KC * f + c - 1)
                    elif after_row is not None:
                        pe.wait_ge(s_qn, KC * (after_row + 1))
                    elif not first:
                        pe.wait_ge(s_t1e, KC * f)
                    for t in range(NT):
                        tp = pe.transpose(t_bank[c % 2][:, t * P:(t + 1) * P],
                                          xnw[:, t * D + c * P:t * D + (c + 1) * P], ident[:])
                    tp.then_inc(s_t1, 1)

            def hidden(f, c, before_in):
                if c == 0:
                    pe.wait_ge(s_sel, f + 1)
                pe.wait_ge(s_t1e, KC * f + c + 1)
                pe.wait_ge(s_xtl, KC * f + c + 1)
                for k in range(TOPK):
                    j = TOPK * c + k
                    if j >= 4:
                        pe.wait_ge(s_gelu, H_JOBS * f + j - 3)
                    elif before_in is not None:
                        pe.wait_ge(s_ina, IN_JOBS * before_in + 17 + j)
                        if j == 2:
                            pe.wait_ge(s_u, KC * (before_in + 1))
                    elif not (isinstance(f, int) and f in (0, B)):
                        pe.wait_ge(s_gelu, H_JOBS * f - 3 + j)
                    mm3(pe, in_bank[j % 4][:], w1_hi[:, k, :], w1_lo[:, k, :], xt_hi[:, c % 2, :],
                        xt_lo[:, c % 2, :], True, True).then_inc(s_h, 1)

            def experts_out(f, c, job):
                pe.wait_ge(s_hl, H_JOBS * f + TOPK * (c + 1))
                if not (isinstance(f, int) and f == 0 and c < 2):
                    pe.wait_ge(s_obf, job + c - 1)
                for k in range(TOPK):
                    mm = mm3(pe, o_bank[c % 2][:], w2_hi[:, k, :], w2_lo[:, k, :], h_hi[:, k, :], h_lo[:, k, :],
                             k == 0, k == TOPK - 1)
                mm.then_inc(s_ob, 1)

            def experts(f, job, before_in):
                hidden(f, 0, before_in)
                hidden(f, 1, before_in)
                experts_out(f, 0, job)
                hidden(f, 2, before_in)
                experts_out(f, 1, job)
                hidden(f, 3, before_in)
                experts_out(f, 2, job)
                experts_out(f, 3, job)

            def project(job, a_hi, a_lo, w_hi, w_lo):
                for t in range(NT):
                    pe.wait_ge(s_obf, job + t - 1)
                    for k in range(KC):
                        tok = slice(t * P, (t + 1) * P)
                        mm = mm3(pe, o_bank[t % 2][:], a_hi[:, k, tok], a_lo[:, k, tok], w_hi[:, k, :],
                                 w_lo[:, k, :], k == 0, k == KC - 1)
                    mm.then_inc(s_ob, 1)

            def w3_part(f, job):
                pe.wait_ge(s_zh, KC * (f + 1))
                pe.wait_ge(s_zl, KC * (f + 1))
                project(job, z_hi, z_lo, w3_hi, w3_lo)

            def t2(b):
                for t in range(NT):
                    pe.wait_ge(s_xn1, NT * b + t + 1)
                    if t >= 2:
                        pe.wait_ge(s_t2a, NT * b + t - 1)
                        pe.wait_ge(s_t2v, NT * b + t - 1)
                    for c in range(KC):
                        tp = pe.transpose(t_bank[t % 2][:, c * P:(c + 1) * P],
                                          xnw[:, t * D + c * P:t * D + (c + 1) * P], ident[:])
                    tp.then_inc(s_t2, 1)

            def in_part(b, first):
                pe.wait_ge(s_t2a, NT * (b + 1))
                pe.wait_ge(s_t2v, NT * (b + 1))
                for c in range(KC):
                    if first:
                        pe.wait_ge(s_whi, 3 + c)
                        if c == 0:
                            pe.wait_ge(s_wlo0, 1)
                        else:
                            pe.wait_ge(s_wlo, 2 + c)
                    for r in range(ROLES):
                        j = ROLES * c + r
                        bank = in_bank[j % 4]
                        if j < 4:
                            pe.wait_ge(s_gelu, H_JOBS * b + 5 + j)
                        else:
                            pe.wait_ge(s_ina, IN_JOBS * b + j - 3)
                            if (j - 4) % ROLES == JOB_V:
                                pe.wait_ge(s_u, KC * b + (j - 4) // ROLES + 1)
                        for k in range(KC):
                            pe.matmul(bank[:], win_hi[:, c, r, k, :], xh[:, k, :], start=(k == 0), stop=False)
                            pe.matmul(bank[:], win_hi[:, c, r, k, :], xl[:, k, :], start=False, stop=False)
                        for k in range(KC):
                            mm = pe.matmul(bank[:], win_lo[:, c, r, k, :], xbf[:, k, :], start=False,
                                           stop=(k == KC - 1))
                        mm.then_inc(s_in, 1)
                        if r == JOB_A:
                            pe.wait_ge(s_sq, KC * b + c + 1)
                            for t in range(NT):
                                mm = pe.matmul(t_bank[0][:, t * HPC:(t + 1) * HPC], q_sq[:, t * P:(t + 1) * P],
                                               head_of[:], start=True, stop=True)
                            mm.then_inc(s_rms, 1)
                    pe.wait_ge(s_rsh, KC * b + c + 1)
                    pe.wait_ge(s_rsl, KC * b + c + 1)
                    if c >= 1:
                        pe.wait_ge(s_qn, KC * b + c)
                    for t in range(NT):
                        cols = slice(t * P, (t + 1) * P)
                        for n, half in enumerate((rs_hi, rs_lo)):
                            flat = half[:].rearrange("p g c -> p (g c)")
                            mm = pe.matmul(t_bank[1][:, cols], flat[:, cols], ident_r[:], start=(n == 0), stop=(n == 1))
                    mm.then_inc(s_rsb, 1)

            def out_part(b, job):
                pe.wait_ge(s_yh, KC * (b + 1))
                pe.wait_ge(s_yl, KC * (b + 1))
                project(job, y_hi, y_lo, wo_hi, wo_lo)

            pe.wait_ge(s_pc, 1)
            route(0)
            t1(0, True, None)
            experts(0, 0, None)
            pe.wait_ge(s_whi, 2)
            pe.wait_ge(s_wlo, 2)
            w3_part(0, 4)
            t2(0)
            in_part(0, True)
            t1(1, False, 0)
            experts(1, ob_expert(1, False), 0)
            out_part(0, ob_out(0))
            w3_part(1, ob_w3(1, False))
            with pe.Fori(1, B - 1) as b:
                t2(b)
                in_part(b, False)
                t1(b + 1, False, b)
                experts(b + 1, ob_expert(b + 1, False), b)
                out_part(b, ob_out(b))
                w3_part(b + 1, ob_w3(b + 1, False))
            t2(B - 1)
            in_part(B - 1, False)
            out_part(B - 1, ob_out(B - 1))
            route(1)
            t1(B, False, B - 1)
            experts(B, ob_expert(B, True), B - 1)
            w3_part(B, ob_w3(B, True))
            with pe.Fori(B + 1, 2 * B) as f:
                t1(f, False, None)
                experts(f, ob_expert(f, True), None)
                w3_part(f, ob_w3(f, True))

        @block.scalar
        def _(act):
            def route_exp(phase):
                act.wait_ge(s_sh, phase + 1)
                act.activation(lg[:], lg[:], ACT.Exp).then_inc(s_exp, 1)

            def t1_out(f, c):
                act.wait_ge(s_t1, KC * f + c + 1)
                if c == 0 and not (isinstance(f, int) and f == 0):
                    act.wait_ge(s_zl, KC * f)
                act.activation(xt[:, c, :], t_bank[c % 2][:], ACT.Copy)
                act.activation(xt_hi[:, c % 2, :], t_bank[c % 2][:], ACT.Copy).then_inc(s_t1e, 1)

            def gelu(f, c):
                for k in range(TOPK):
                    act.wait_ge(s_h, H_JOBS * f + TOPK * c + k + 1)
                    if not (isinstance(f, int) and f == 0 and c == 0):
                        act.wait_ge(s_hl, H_JOBS * f + TOPK * (c - 1) + k + 1)
                    act.activation(hf[:, k, :], in_bank[(TOPK * c + k) % 4][:], ACT.Gelu,
                                   bias=w1_sel[:, k, HD:FB]).then_inc(s_gelu, 1)

            def z_out(f, c, job):
                act.wait_ge(s_obf, job + c + 1)
                act.activation(z_hi[:, c, :], xt[:, c, :], ACT.Copy).then_inc(s_zh, 1)

            def ffn(f, job):
                t1_out(f, 0)
                t1_out(f, 1)
                gelu(f, 0)
                t1_out(f, 2)
                gelu(f, 1)
                t1_out(f, 3)
                gelu(f, 2)
                z_out(f, 0, job)
                gelu(f, 3)
                for c in range(1, KC):
                    z_out(f, c, job)

            def t2_out(b):
                for t in range(NT):
                    act.wait_ge(s_t2, NT * b + t + 1)
                    src = t_bank[t % 2][:].rearrange("p (c s) -> p c s", c=KC)
                    cols = slice(t * P, (t + 1) * P)
                    act.activation(xh[:, :, cols], src, ACT.Copy)
                    act.activation(xbf[:, :, cols], src, ACT.Copy).then_inc(s_t2a, 1)

            def group(b, c):
                def bank(r):
                    act.wait_ge(s_in, IN_JOBS * b + ROLES * c + r + 1)
                    return in_bank[(ROLES * c + r) % 4][:]

                def y_out(c):
                    act.wait_ge(s_y, KC * b + c + 1)
                    act.activation(y_hi[:, c, :], qt[:], ACT.Copy).then_inc(s_yh, 1)

                src = bank(JOB_Q)
                if c >= 1:
                    act.wait_ge(s_rms, KC * b + c)
                act.activation(q_sq[:], src, ACT.Square).then_inc(s_sq, 1)
                if c >= 1:
                    y_out(c - 1)
                    act.wait_ge(s_yl, KC * b + c)
                act.activation(qt[:], src, ACT.Copy).then_inc(s_ina, 1)
                src = bank(JOB_A)
                if c >= 1:
                    act.wait_ge(s_qm, KC * b + c)
                act.activation(decay[:], src, ACT.Sigmoid, bias=two[:]).then_inc(s_ina, 1)
                src = bank(JOB_K)
                act.activation(kt[:], src, ACT.Tanh).then_inc(s_ina, 1)
                src = bank(JOB_V)
                if c >= 1:
                    act.wait_ge(s_y, KC * b + c)
                act.activation(vt[:], src, ACT.Copy).then_inc(s_ina, 1)
                src = bank(JOB_G)
                act.activation(gt[:], src, ACT.Sigmoid).then_inc(s_ina, 1)
                if c == KC - 1:
                    y_out(c)

            def attention(b):
                t2_out(b)
                for c in range(KC):
                    group(b, c)

            def split_hi(i, dst, src, scale=1.0):
                act.wait_ge(s_raw[i], 16)
                act.activation(dst, src, ACT.Copy, scale=scale).then_inc(s_whi, 1)

            route_exp(0)
            split_hi(0, w3_hi[:].rearrange("p k n -> p (k n)"), raw[:, 0, 0:KC * D], 0.5)
            split_hi(1, wo_hi[:].rearrange("p k n -> p (k n)"), raw[:, 1, 0:KC * D])
            split_hi(2, win_hi[:, 0].rearrange("p r k n -> p (r k n)"), raw[:, 2, :])
            act.wait_ge(s_pc, 1)
            act.wait_ge(s_sel, 1)
            ffn(0, 0)
            for g in range(1, KC):
                split_hi(2 + g, win_hi[:, g].rearrange("p r k n -> p (r k n)"), raw[:, (g + 2) % 3, :])
            with act.Fori(0, B - 1) as b:
                attention(b)
                ffn(b + 1, ob_expert(b + 1, False))
            attention(B - 1)
            route_exp(1)
            with act.Fori(B, 2 * B) as f:
                ffn(f, ob_expert(f, True))

        @block.gpsimd
        def _(pool):
            own = Steps(pool, s_po)
            own.mark(pool.memset(ident[:], 0.0))
            own.mark(pool.memset(diag[:], 0.0))
            own.mark(pool.memset(head_of[:], 1.0))
            own.mark(pool.memset(neg_half[:], -0.5))
            own.mark(pool.memset(two[:], 2.0))
            own.mark(pool.memset(ones[:], 1.0))
            own.do(pool.memset(starts[:], 0.0)) if False else None
            for e in range(E):
                own.mark(pool.memset(rank[:, e:e + 1], float(E - e)))
            own.wait(own.n)
            own.mark(pool.affine_select(out=ident[:], in_=ident[:], compare_op=ALU.not_equal, fill=1.0, base=0,
                                        pattern=[[-1, P]], channel_multiplier=1))
            for j in range(HPC):
                own.do(pool.affine_select(out=diag[:], in_=diag[:], compare_op=ALU.not_equal, fill=1.0,
                                          base=-HD * j, pattern=[[-1, HD]], channel_multiplier=1))
            own.do(pool.affine_select(out=head_of[:], in_=head_of[:], compare_op=ALU.is_ge, fill=0.0, base=0,
                                      pattern=[[-HD, HPC]], channel_multiplier=1))
            pool.affine_select(out=head_of[:], in_=head_of[:], compare_op=ALU.is_ge, fill=0.0, base=HD - 1,
                               pattern=[[HD, HPC]], channel_multiplier=-1).then_inc(s_pc, 1)

            def route_rstd(phase):
                for t in range(NT):
                    pool.wait_ge(s_rv, NT * phase + t + 1)
                    pool.tensor_tensor(rstd[:, :, t], mv[:, :, t, 1], neg_half[:, 0:B], ALU.pow).then_inc(s_rp, 1)

            def ffn(f, job, late, row):
                def xt_split(c):
                    pool.wait_ge(s_t1e, KC * f + c + 1)
                    if c >= 2:
                        pool.wait_ge(s_h, H_JOBS * f + TOPK * (c - 1))
                    pool.tensor_tensor(xt_lo[:, c % 2, :], xt[:, c, :], xt_hi[:, c % 2, :],
                                       ALU.subtract).then_inc(s_xtl, 1)

                def z_split(c):
                    pool.wait_ge(s_zh, KC * f + c + 1)
                    pool.tensor_tensor(z_lo[:, c, :], xt[:, c, :], z_hi[:, c, :], ALU.subtract).then_inc(s_zl, 1)

                xt_split(0)
                xt_split(1)
                xt_split(2)
                xt_split(3)
                for c in range(KC):
                    z_split(c)

            def residual_bias(f):
                pool.wait_ge(s_xn, NT * (f + 1))
                for t in range(NT):
                    pool.tensor_tensor(xa[:, t, :], xa[:, t, :], b3_half[:], ALU.add).then_inc(s_xb, 1)

            def ln_rstd(b):
                for t in range(NT):
                    pool.wait_ge(s_v1, NT * b + t + 1)
                    pool.tensor_tensor(rstd1[:, t:t + 1], mv1[:, t, 1:2], neg_half[:, 0:1],
                                       ALU.pow).then_inc(s_p1, 1)

            def group(b, c):
                pool.wait_ge(s_ms, KC * b + c + 1)
                pool.tensor_tensor(rs[:], ms[:], neg_half[:], ALU.pow).then_inc(s_rsp, 1)
                pool.wait_ge(s_rsp, KC * b + c + 1)
                pool.wait_ge(s_rsh, KC * b + c + 1)
                pool.tensor_tensor(rs_lo[:], rs[:].unsqueeze(2).to_broadcast([P, NT * HPC, HD]), rs_hi[:],
                                   ALU.subtract).then_inc(s_rsl, 1)
                pool.wait_ge(s_qm, KC * b + c + 1)
                pool.wait_ge(s_ina, IN_JOBS * b + ROLES * c + JOB_V + 1)
                pool.tensor_tensor(qt[:], qt[:], vt[:], ALU.subtract).then_inc(s_pd, 1)
                pool.wait_ge(s_pd, 2 * (KC * b + c) + 1)
                pool.wait_ge(s_ina, IN_JOBS * b + ROLES * c + JOB_G + 1)
                pool.tensor_tensor(qt[:], qt[:], gt[:], ALU.mult).then_inc(s_pd, 1)
                pool.wait_ge(s_pd, 2 * (KC * b + c) + 2)
                pool.tensor_tensor(qt[:], qt[:], vt[:], ALU.add).then_inc(s_y, 1)
                pool.wait_ge(s_yh, KC * b + c + 1)
                pool.tensor_tensor(y_lo[:, c, :], qt[:], y_hi[:, c, :], ALU.subtract).then_inc(s_yl, 1)

            route_rstd(0)
            pool.wait_ge(s_rm, NT)
            pool.wait_ge(s_whi, 3)
            pool.tensor_tensor(win_lo[:, 0].rearrange("p r k n -> p (r k n)"), raw[:, 2, :],
                               win_hi[:, 0].rearrange("p r k n -> p (r k n)"), ALU.subtract).then_inc(s_wlo0, 1)
            ffn(0, 0, False, 0)
            pool.wait_ge(s_vc, 2)
            residual_bias(0)
            ln_rstd(0)
            with pool.Fori(0, B - 1) as b:
                for c in range(KC):
                    group(b, c)
                ffn(b + 1, 0, False, 0)
                residual_bias(b + 1)
                ln_rstd(b + 1)
            for c in range(KC):
                group(B - 1, c)
            route_rstd(1)
            with pool.Fori(B, 2 * B) as f:
                ffn(f, 0, True, 0)
                residual_bias(f)

        @block.vector
        def _(ve):
            own = Steps(ve, s_ve)

            def route(phase):
                for t in range(NT):
                    src = xa if t % 2 == 0 else x1
                    xn = xnw if t % 2 == 0 else xnr
                    ve.wait_ge(s_xr[t % 2], 16 * (2 * phase + t // 2 + 1))
                    for b in range(B):
                        m = own.mark(ve.bn_stats(stats[:, b, :], src[:, b, :]))
                    own.wait(m)
                    for b in range(B):
                        m = own.mark(ve.bn_aggr(mv[:, b, t, :], stats[:, b, :]))
                    own.wait(m)
                    ve.tensor_scalar(mv[:, :, t, 1], mv[:, :, t, 1], LN_EPS, None, ALU.add).then_inc(s_rv, 1)
                    ve.wait_ge(s_rp, NT * phase + t + 1)
                    if t >= 2:
                        ve.wait_ge(s_rm, NT * phase + t - 1)
                    for b in range(B):
                        dst = xn[:].rearrange("p (d b c) -> p d b c", b=B, c=HD)[:, :, b, :]
                        ins = ve.tensor_scalar(dst, src[:, b, :].rearrange("p (d c) -> p d c", c=HD),
                                               mv[:, b, t, 0:1], rstd[:, b, t:t + 1], ALU.subtract, ALU.mult)
                    ins.then_inc(s_rn, 1)

            def choose(phase):
                def over_e(ap):
                    return ap.unsqueeze(2).to_broadcast([P, B, E])

                ve.wait_ge(s_rm, NT * (phase + 1))
                acc = o_bank[0][:, 0:E * HD].rearrange("p (e c) -> p e c", e=E)
                scratch = prod[:].rearrange("p k f e -> p (k f e)")[:, 0:E * HD].rearrange("p (e c) -> p e c", e=E)
                own.do(ve.tensor_tensor(scratch, acc, diag[:].unsqueeze(1).to_broadcast([P, E, HD]), ALU.mult))
                own.do(ve.tensor_reduce(part[:], scratch, AX.X, ALU.add))
                ve.tensor_tensor(lmix[:], part[:].unsqueeze(1).to_broadcast([P, B, E]), over_e(head_of[:]),
                                 ALU.mult).then_inc(s_mix, 1)
                ve.wait_ge(s_lg, phase + 1)
                own.do(ve.tensor_tensor(lg[:], o_bank[1][:, 0:B * E].rearrange("p (b e) -> p b e", b=B),
                                        sw_bias[:].unsqueeze(1).to_broadcast([P, B, E]), ALU.add))
                own.do(ve.tensor_reduce(red[:], lg[:], AX.X, ALU.max))
                ve.tensor_tensor(lg[:], lg[:], over_e(red[:]), ALU.subtract).then_inc(s_sh, 1)
                ve.wait_ge(s_exp, phase + 1)
                own.do(ve.tensor_reduce(red[:], lg[:], AX.X, ALU.add))
                own.do(ve.reciprocal(red2[:], red[:]))
                own.do(ve.tensor_tensor(lg[:], lg[:], over_e(red2[:]), ALU.mult))
                for k in range(TOPK):
                    own.do(ve.tensor_reduce(gates[:, :, k], lg[:], AX.X, ALU.max))
                    own.do(ve.tensor_tensor(eq[:], lg[:], over_e(gates[:, :, k]), ALU.is_equal))
                    own.do(ve.tensor_tensor(eq[:], eq[:], rank[:].unsqueeze(1).to_broadcast([P, B, E]), ALU.mult))
                    own.do(ve.tensor_reduce(red[:], eq[:], AX.X, ALU.max))
                    own.do(ve.tensor_tensor(pick[:, :, k, :], eq[:], over_e(red[:]), ALU.is_equal))
                    m = own.mark(ve.tensor_tensor(pick_g[:, :, k, :], pick[:, :, k, :], over_e(gates[:, :, k]),
                                                  ALU.mult))
                    if k == 0:
                        m = own.mark(ve.scalar_tensor_tensor(out=lg[:], in0=pick[:, :, 0, :], scalar=-2.0,
                                                             in1=lg[:], op0=ALU.mult, op1=ALU.add))
                    own.wait(m)

            def select(row, f):
                for tab, choice, sel, hi, lo in ((w1_tab, pick, w1_sel, w1_hi, w1_lo),
                                                 (w2_tab, pick_g, w2_sel, w2_hi, w2_lo)):
                    for k in range(TOPK):
                        m = own.mark(ve.tensor_tensor(
                            prod[:, k], tab[:],
                            choice[:, bass.ds(row, 1), k, :].to_broadcast([P, FB, E]), ALU.mult))
                    own.wait(m)
                    own.do(ve.tensor_reduce(sel[:], prod[:], AX.X, ALU.add))
                    for k in range(TOPK):
                        m = own.mark(ve.tensor_tensor(
                            w_diag[:, k], sel[:, k, 0:HD].unsqueeze(1).to_broadcast([P, HPC, HD]),
                            head_of[:].unsqueeze(2).to_broadcast([P, HPC, HD]), ALU.mult))
                    own.wait(m)
                    own.do(ve.tensor_copy(hi[:].rearrange("p k (j c) -> p k j c", j=HPC), w_diag[:]))
                    own.do(ve.tensor_tensor(lo[:].rearrange("p k (j c) -> p k j c", j=HPC), w_diag[:],
                                            hi[:].rearrange("p k (j c) -> p k j c", j=HPC), ALU.subtract))
                ve.tensor_tensor(b2_col[:], w2_sel[:, 0, HD:FB], w2_sel[:, 1, HD:FB], ALU.add).then_inc(s_sel, 1)
                ve.wait_ge(s_sel, f + 1)

            def normalise(f, row):
                ve.wait_ge(s_xa, 16 * (f + 1))
                for t in range(NT):
                    ve.tensor_scalar(xnw[:, t * D:(t + 1) * D], xa[:, t, :], mv[:, bass.ds(row, 1), t, 0],
                                     rstd[:, bass.ds(row, 1), t], ALU.subtract, ALU.mult).then_inc(s_xn, 1)

            def split_hidden(f, c, job):
                for k in range(TOPK):
                    ve.wait_ge(s_gelu, H_JOBS * f + TOPK * c + k + 1)
                    if c >= 1 and k == 0:
                        ve.wait_ge(s_ob, job + c)
                    own.do(ve.tensor_copy(h_hi[:, k, :], hf[:, k, :]))
                    ve.tensor_tensor(h_lo[:, k, :], hf[:, k, :], h_hi[:, k, :], ALU.subtract).then_inc(s_hl, 1)

            def add_experts(c, job):
                ve.wait_ge(s_ob, job + c + 1)
                ve.scalar_tensor_tensor(out=xt[:, c, :], in0=o_bank[c % 2][:], scalar=b2_col[:], in1=xt[:, c, :],
                                        op0=ALU.add, op1=ALU.add).then_inc(s_obf, 1)

            def experts(f, job, extra):
                split_hidden(f, 0, job)
                for c in range(KC):
                    if c < KC - 1:
                        split_hidden(f, c + 1, job)
                    add_experts(c, job)
                    extra(c)

            def w3_add(f, job, t):
                ve.wait_ge(s_xb, NT * f + t + 1)
                ve.wait_ge(s_ob, job + t + 1)
                return ve.tensor_tensor(x1[:, t, :], o_bank[t % 2][:], xa[:, t, :], ALU.add)

            def w3_norm(f, job):
                def norm(t):
                    ve.wait_ge(s_p1, NT * f + t + 1)
                    ve.tensor_scalar(xnw[:, t * D:(t + 1) * D], x1[:, t, :], mv1[:, t, 0:1], rstd1[:, t:t + 1],
                                     ALU.subtract, ALU.mult).then_inc(s_xn1, 1)

                if not (isinstance(f, int) and f == 0):
                    ve.wait_ge(s_x2, 16 * NT * f)
                ve.wait_ge(s_t1, KC * (f + 1))
                for t in range(NT):
                    w3_add(f, job, t).then_inc(s_obf, 1)
                    ve.wait_ge(s_obf, job + t + 1)
                    own.do(ve.bn_stats(stats[:, t, :], x1[:, t, :]))
                    ve.tensor_copy(fence[:], neg_half[:, 0:1])
                    own.do(ve.bn_aggr(mv1[:, t, :], stats[:, t, :]))
                    ve.tensor_scalar(mv1[:, t, 1:2], mv1[:, t, 1:2], LN_EPS, None, ALU.add).then_inc(s_v1, 1)
                    if t >= 1:
                        norm(t - 1)
                norm(NT - 1)

            def t2_lo(b):
                for t in range(NT):
                    ve.wait_ge(s_t2a, NT * b + t + 1)
                    cols = slice(t * P, (t + 1) * P)
                    ve.tensor_tensor(xl[:, :, cols], t_bank[t % 2][:].rearrange("p (c s) -> p c s", c=KC),
                                     xh[:, :, cols], ALU.subtract).then_inc(s_t2v, 1)

            def group(b, c):
                job = IN_JOBS * b + ROLES * c
                ve.wait_ge(s_rms, KC * b + c + 1)
                ve.tensor_scalar(ms[:], t_bank[0][:, 0:NT * HPC], 1.0 / HD, RMS_EPS, ALU.mult,
                                 ALU.add).then_inc(s_ms, 1)
                ve.wait_ge(s_ina, job + JOB_A + 1)
                own.do(ve.tensor_scalar(decay[:], decay[:], A_MIN, A_MAX, ALU.max, ALU.min))
                first = decay[:].rearrange("p (n s) -> p n s", s=CHUNK)[:, :, 0:1]
                own.do(ve.tensor_scalar(starts[:].rearrange("p (n s) -> p n s", s=CHUNK)[:, :, 0:1], first,
                                        1.0 / GUARD, None, ALU.mult))
                pref_done = own.mark(ve.tensor_tensor_scan(pref[:], decay[:], starts[:], 0.0, ALU.mult, ALU.max))
                ve.wait_ge(s_rsp, KC * b + c + 1)
                ve.tensor_copy(rs_hi[:], rs[:].unsqueeze(2).to_broadcast([P, NT * HPC, HD])).then_inc(s_rsh, 1)
                ve.wait_ge(s_in, job + JOB_V + 1)
                ve.wait_ge(s_ina, job + JOB_V + 1)
                ve.tensor_tensor(kt[:], kt[:], in_bank[(ROLES * c + JOB_V) % 4][:], ALU.mult).then_inc(s_u, 1)
                ve.wait_ge(s_u, KC * b + c + 1)
                own.wait(pref_done)
                own.do(ve.scalar_tensor_tensor(out=pref[:], in0=pref[:], scalar=1.0, in1=kt[:], op0=ALU.min,
                                               op1=ALU.mult))
                mem_done = own.mark(ve.tensor_tensor_scan(kt[:], decay[:], pref[:], 0.0, ALU.mult, ALU.add))
                ve.wait_ge(s_rsb, KC * b + c + 1)
                ve.tensor_tensor(qt[:], qt[:], t_bank[1][:], ALU.mult).then_inc(s_qn, 1)
                ve.wait_ge(s_qn, KC * b + c + 1)
                own.wait(mem_done)
                ve.tensor_tensor(qt[:], qt[:], kt[:], ALU.mult).then_inc(s_qm, 1)

            def out_add(b, job):
                for t in range(NT):
                    ve.wait_ge(s_ob, job + t + 1)
                    ve.tensor_tensor(x1[:, t, :], x1[:, t, :], o_bank[t % 2][:], ALU.add).then_inc(s_obf, 1)
                    ve.wait_ge(s_obf, job + t + 1)
                    ve.tensor_copy(red[:, 0:1], x1[:, t, 0:1]).then_inc(s_xo, 1)
                    ve.wait_ge(s_xo, NT * b + t + 1)

            def split_lo(i, dst, src, hi, scale=None):
                ve.wait_ge(s_whi, i + 1)
                if scale is None:
                    ins = ve.tensor_tensor(dst, src, hi, ALU.subtract)
                else:
                    ins = ve.scalar_tensor_tensor(out=dst, in0=src, scalar=scale, in1=hi, op0=ALU.mult,
                                                  op1=ALU.subtract)
                ins.then_inc(s_wlo, 1)

            def split_group(c):
                if 1 <= c + 1 < KC:
                    g = c + 1
                    split_lo(2 + g, win_lo[:, g].rearrange("p r k n -> p (r k n)"), raw[:, (g + 2) % 3, :],
                             win_hi[:, g].rearrange("p r k n -> p (r k n)"))

            ve.memset(ones[:], 1.0) if False else None
            ve.wait_ge(s_pc, 1)
            ve.tensor_copy(ident_r[:], ident[:]).then_inc(s_vc, 1)
            ve.wait_ge(s_small, 16 * 6)
            ve.tensor_scalar(b3_half[:], b3_half[:], 0.5, None, ALU.mult).then_inc(s_vc, 1)
            route(0)
            choose(0)
            select(0, 0)
            ve.wait_ge(s_rm, NT)
            normalise(0, 0)
            split_lo(0, w3_lo[:].rearrange("p k n -> p (k n)"), raw[:, 0, 0:KC * D],
                     w3_hi[:].rearrange("p k n -> p (k n)"), 0.5)
            split_lo(1, wo_lo[:].rearrange("p k n -> p (k n)"), raw[:, 1, 0:KC * D],
                     wo_hi[:].rearrange("p k n -> p (k n)"))
            experts(0, 0, lambda c: None)
            w3_norm(0, 4)
            for g in range(1, KC):
                split_group(g - 1)
            ve.wait_ge(s_wlo, 5)
            own.do(ve.memset(starts[:], 0.0))

            per_row = 0
            base = own.base + own.n

            def attention(b, before):
                t2_lo(b)
                group(b, 0)
                before(0)
                group(b, 1)
                before(1)
                group(b, 2)
                group(b, 3)

            def next_row(b):
                def before(c):
                    if c == 0:
                        select(b + 1, b + 1)
                    else:
                        normalise(b + 1, b + 1)
                return before

            with ve.Fori(0, B - 1) as b:
                own.base, own.n = base + b * VE_ROW_STEPS, 0
                attention(b, next_row(b))
                experts(b + 1, ob_expert(b + 1, False), lambda c: None)
                out_add(b, ob_out(b))
                w3_norm(b + 1, ob_w3(b + 1, False))
                assert own.n == VE_ROW_STEPS, own.n
            own.base, own.n = base + (B - 1) * VE_ROW_STEPS, 0
            attention(B - 1, lambda c: None)
            out_add(B - 1, ob_out(B - 1))
            route(1)
            choose(1)
            base2 = own.base + own.n

            def late(f, row):
                select(row, f)
                normalise(f, row)
                experts(f, ob_expert(f, True), lambda c: None)
                if not (isinstance(f, int) and f == B):
                    ve.wait_ge(s_out, 16 * NT * (f - B))
                for t in range(NT):
                    w3_add(f, ob_w3(f, True), t).then_inc(s_obf, 1)
                    ve.wait_ge(s_obf, ob_w3(f, True) + t + 1)
                    ve.tensor_copy(red[:, 0:1], x1[:, t, 0:1]).then_inc(s_fin, 1)
                    ve.wait_ge(s_fin, NT * (f - B) + t + 1)

            own.base, own.n = base2, 0
            ve.wait_ge(s_rm, 2 * NT)
            late(B, 0)
            assert own.n == VE_LATE_STEPS, own.n
            with ve.Fori(1, B) as row:
                own.base, own.n = base2 + row * VE_LATE_STEPS, 0
                late(row + B, row)


VE_ROW_STEPS = 50
VE_LATE_STEPS = 22


_ORDER = ["q", "a", "k", "v", "g"]


def kernel(**inputs):
    import numpy as np
    import concourse.bacc as bacc
    from concourse.bass_utils import run_bass_kernel_spmd

    a = {k.replace("L0_attn_", "").replace("L0_ffn_", ""): np.asarray(v) for k, v in inputs.items()}
    w_in = a["w_in"].reshape(5, KC, P, KC, P)[[0, 3, 1, 2, 4]].transpose(1, 4, 0, 3, 2)
    arrays = {
        "x": a["x"],
        "w_in": w_in.reshape(KC, P, ROLES * KC * P),
        "w_out": a["w_out"].T.reshape(KC, P, D).transpose(1, 0, 2),
        "switch_w": a["switch_w"].reshape(E, NT, P, D).transpose(2, 1, 0, 3),
        "switch_b": a["switch_b"],
        "w1": a["w1"].transpose(2, 1, 0),
        "b1": a["b1"].T,
        "w2": a["w2"].transpose(2, 1, 0),
        "b2": a["b2"].T,
        "w3": a["w3"].T.reshape(KC, P, D).transpose(1, 0, 2),
        "b3": a["b3"],
    }
    nc = bacc.Bacc("TRN2", target_bir_lowering=False, num_devices=1)
    feed, args = {}, []
    for name, arr in arrays.items():
        arr = np.ascontiguousarray(arr)
        feed[f"in_{name}"] = arr
        args.append(nc.dram_tensor(f"in_{name}", arr.shape, mybir.dt.from_np(arr.dtype), kind="ExternalInput").ap())
    args.append(nc.dram_tensor("out_0", (B, S, D), F32, kind="ExternalOutput").ap())
    macaron_kernel(nc, *args)
    r = run_bass_kernel_spmd(nc, [feed], core_ids=[0])
    return r.results[0]["out_0"]
```

```python
from contextlib import ExitStack

import concourse.bass as bass
from concourse import mybir

P = 128
ALU = mybir.AluOpType
ACT = mybir.ActivationFunctionType
AX = mybir.AxisListType
F32 = mybir.dt.float32
F32R = mybir.dt.float32r
BF16 = mybir.dt.bfloat16

B, S, D = 4, 512, 512
NT = S // P
KC = D // P
E, TOPK = 8, 2
HD = 32
HPC = P // HD
CHUNK = 64
ROLES = 5
GUARD = 1e-6
LN_EPS = 1e-5
RMS_EPS = 1.1920928955078125e-07
A_MIN, A_MAX = 0.6, 0.9995
FB = HD + 1


JOB_Q, JOB_A, JOB_K, JOB_V, JOB_G = range(ROLES)
IN_JOBS = ROLES * KC
H_JOBS = TOPK * KC


class Steps:

    def __init__(self, eng, sem):
        self.eng, self.sem, self.base, self.n = eng, sem, 0, 0

    def mark(self, ins):
        self.n += 1
        ins.then_inc(self.sem, 1)
        return self.base + self.n

    def wait(self, value):
        self.eng.wait_ge(self.sem, value)

    def do(self, ins):
        self.wait(self.mark(ins))


def macaron_kernel(nc, x, w_in, w_out, switch_w, switch_b, w1, b1, w2, b2, w3, b3, out):
    x2_dram = nc.dram_tensor("x2_dram", (B, S, D), F32).ap()

    with ExitStack() as ctx:
        def sb(name, shape, dt=F32, into=ctx):
            return into.enter_context(nc.sbuf_tensor(name, shape, dt))

        def sem(name):
            return ctx.enter_context(nc.semaphore(name))

        with ExitStack() as region:
            route_w = sb("route_w", [P, NT, E, D], into=region)
        with ExitStack() as region:
            z_hi1 = sb("z_hi1", [P, KC, S], F32R, into=region)
            z_lo1 = sb("z_lo1", [P, KC, S], F32R, into=region)
            xa1 = sb("xa1", [P, NT, D], into=region)
            hf1 = sb("hf1", [P, TOPK, S], into=region)
            h_hi1 = sb("h_hi1", [P, TOPK, S], F32R, into=region)
            h_lo1 = sb("h_lo1", [P, TOPK, S], F32R, into=region)
            sel1 = [sb(n, [P, TOPK, FB], into=region) for n in ("w1_sel1", "w2_sel1")]
            w_hi1 = [sb(n, [P, TOPK, P], F32R, into=region) for n in ("w1_hi1", "w2_hi1")]
            w_lo1 = [sb(n, [P, TOPK, P], F32R, into=region) for n in ("w1_lo1", "w2_lo1")]
            b2_col1 = sb("b2_col1", [P, 1], into=region)
        win_hi = sb("win_hi", [P, KC, ROLES, KC, P], F32R)
        win_lo = sb("win_lo", [P, KC, ROLES, KC, P], BF16)
        gt = sb("gt", [P, S])
        starts = sb("starts", [P, S])

        w3_hi = sb("w3_hi", [P, KC, D], F32R)
        w3_lo = sb("w3_lo", [P, KC, D], F32R)
        wo_hi = sb("wo_hi", [P, KC, D], F32R)
        wo_lo = sb("wo_lo", [P, KC, D], F32R)
        xa = sb("xa", [P, NT, D])
        x1 = sb("x1", [P, NT, D])
        xnw = sb("xnw", [P, NT * D])
        with ExitStack() as region:
            xnr = sb("xnr", [P, NT * D], into=region)
        z_lo = sb("z_lo", [P, KC, S], F32R)

        with ExitStack() as region:
            xh = sb("xh", [P, KC, S], F32R, into=region)
            xl = sb("xl", [P, KC, S], F32R, into=region)
            xbf = sb("xbf", [P, KC, S], BF16, into=region)
            prod = sb("prod", [P, TOPK, FB, E], into=region)
            w_diag = sb("w_diag", [P, TOPK, HPC, HD], into=region)
            gv = sb("gv", [P, S], into=region)
            sb("r1_pad", [P, 2048 - TOPK * FB * E - TOPK * P - S], into=region)
            pref = sb("pref", [P, S], into=region)
            kt = sb("kt", [P, S], into=region)
            vt = sb("vt", [P, S], into=region)
            rs_wide = sb("rs_wide", [P, NT, HPC, HD], into=region)
        xt = sb("xt", [P, KC, S])
        xt_hi = sb("xt_hi", [P, 2, S], F32R)
        xt_lo = sb("xt_lo", [P, 2, S], F32R)
        hf = sb("hf", [P, TOPK, S])
        h_hi = sb("h_hi", [P, TOPK, S], F32R)
        h_lo = sb("h_lo", [P, TOPK, S], F32R)
        z_hi = sb("z_hi", [P, KC, S], F32R)

        with ExitStack() as region:
            raw = sb("raw", [P, 3, ROLES * KC * P], into=region)
        y_hi = sb("y_hi", [P, KC, S], F32R)
        y_lo = sb("y_lo", [P, KC, S], F32R)
        decay = sb("decay", [P, S])
        qt = sb("qt", [P, S])
        q_sq = sb("q_sq", [P, S])
        yt = sb("yt", [P, S])
        x1p = sb("x1p", [P, NT, D])

        ident = sb("ident", [P, P])
        ones = sb("ones", [P, P])
        head_of = sb("head_of", [P, HPC])
        diag = sb("diag", [P, HD])
        tab = [sb(n, [P, FB, E]) for n in ("w1_tab", "w2_tab")]
        sel0 = [sb(n, [P, TOPK, FB]) for n in ("w1_sel", "w2_sel")]
        w_hi0 = [sb(n, [P, TOPK, P], F32R) for n in ("w1_hi", "w2_hi")]
        w_lo0 = [sb(n, [P, TOPK, P], F32R) for n in ("w1_lo", "w2_lo")]
        b2_col0 = sb("b2_col", [P, 1])
        b3_half = sb("b3_half", [P, D])
        sw_bias = sb("sw_bias", [P, E])
        stats = sb("stats", [P, NT, 6])
        mv = sb("mv", [P, B, NT, 2])
        rstd = sb("rstd", [P, B, NT])
        mv1 = sb("mv1", [P, NT, 2])
        rstd1 = sb("rstd1", [P, NT])
        neg_half = sb("neg_half", [P, NT * HPC])
        ms = sb("ms", [P, NT * HPC])
        rs = sb("rs", [P, NT * HPC])
        two = sb("two", [P, 1])
        rms_eps = sb("rms_eps", [P, 1])
        part = sb("part", [P, E])
        lmix = sb("lmix", [P, B, E])
        lg = sb("lg", [P, B, E])
        eq = sb("eq", [P, B, E])
        rank = sb("rank", [P, E])
        red = sb("red", [P, B])
        red2 = sb("red2", [P, B])
        fence = sb("fence", [P, 1])
        gates = sb("gates", [P, B, TOPK])
        pick = sb("pick", [P, B, TOPK, E])
        pick_g = sb("pick_g", [P, B, TOPK, E])

        ffn0 = dict(z_hi=z_hi, z_lo=z_lo, sel=sel0, w_hi=w_hi0, w_lo=w_lo0, b2=b2_col0)
        ffn1 = dict(z_hi=z_hi1, z_lo=z_lo1, sel=sel1, w_hi=w_hi1, w_lo=w_lo1, b2=b2_col1)
        hid0 = (hf, h_hi, h_lo)
        hid1 = (hf1, h_hi1, h_lo1)

        def ffn_set(f):
            return ffn1 if isinstance(f, int) and f > B and f % 2 else ffn0

        def ffn_input(f):
            if isinstance(f, int) and f > B:
                return ((xa1, s_xa1, 16), (x1p, s_xa2, 16), (xa, s_xa, 16 * (B + 2)))[f - B - 1]
            return xa, s_xa, 16 * (f + 1)

        def hid_set(f, c):
            return hid1 if isinstance(f, int) and f >= B and c % 2 else hid0

        banks = [ctx.enter_context(nc.psum_tensor(f"bank{i}", [P, 512], F32)) for i in range(8)]
        in_bank = banks[0:4]
        t_bank = banks[4:6]
        o_bank = banks[6:8]

        s_small = sem("s_small")
        s_xr = [sem(f"s_xr{i}") for i in range(2)]
        s_sw = [sem(f"s_sw{t}") for t in range(NT)]
        s_xa = sem("s_xa")
        s_xa1 = sem("s_xa1")
        s_xa2 = sem("s_xa2")
        s_raw = [sem(f"s_raw{i}") for i in range(6)]
        s_x2 = sem("s_x2")
        s_out = [sem(f"s_out{t}") for t in range(NT)]
        s_pc = sem("s_pc")
        s_vc = sem("s_vc")
        s_whi = sem("s_whi")
        s_wlo = sem("s_wlo")
        s_wlp = sem("s_wlp")
        s_rv = sem("s_rv")
        s_rp = sem("s_rp")
        s_rn = sem("s_rn")
        s_rm = sem("s_rm")
        s_mix = sem("s_mix")
        s_lg = sem("s_lg")
        s_sh = sem("s_sh")
        s_exp = sem("s_exp")
        s_sel = [sem("s_sel1"), sem("s_sel2")]
        s_xn = sem("s_xn")
        s_xb = sem("s_xb")
        s_t1 = sem("s_t1")
        s_t1e = sem("s_t1e")
        s_xtl = sem("s_xtl")
        s_h = sem("s_h")
        s_gelu = sem("s_gelu")
        s_hl = sem("s_hl")
        s_ob = sem("s_ob")
        s_obf = sem("s_obf")
        s_zh = sem("s_zh")
        s_zl = sem("s_zl")
        s_v1 = sem("s_v1")
        s_p1 = sem("s_p1")
        s_xn1 = sem("s_xn1")
        s_t2 = sem("s_t2")
        s_t2a = sem("s_t2a")
        s_t2v = sem("s_t2v")
        s_in = sem("s_in")
        s_ina = sem("s_ina")
        s_u = sem("s_u")
        s_sq = sem("s_sq")
        s_ms = sem("s_ms")
        s_mse = sem("s_mse")
        s_rs = sem("s_rs")
        s_rsw = sem("s_rsw")
        s_rst = sem("s_rst")
        s_qn = sem("s_qn")
        s_qm = sem("s_qm")
        s_gv = sem("s_gv")
        s_w = sem("s_w")
        s_y = sem("s_y")
        s_yh = sem("s_yh")
        s_yl = sem("s_yl")
        s_ve = sem("s_ve")
        s_po = sem("s_po")

        FIRST = ["O0", "O1", "O2", "O3", "W0", "W1", "W2", "W3"]
        ROW = ["A0", "A1", "O0", "O1", "O2", "A2", "O3", "W0", "W1", "W2", "W3", "A3"]
        row_base = len(FIRST)
        last_base = row_base + (B - 1) * len(ROW)
        late_base = last_base + NT

        def job_first(name):
            return FIRST.index(name)

        def job_row(b, name):
            return b * len(ROW) + (row_base + ROW.index(name))

        def job_last(name):
            return last_base + int(name[1])

        def job_late(f, name):
            n, r = int(name[1]), f - B
            if name[0] == "O":
                return late_base + (n if r == 0 else KC + 8 * (r - 1) + 2 * n + 1)
            return late_base + KC + (8 * r + 2 * n if r < B - 1 else 8 * (B - 1) + n)

        EVENTS = [(0, t, 0, B) for t in range(NT)]
        EVENTS += [(1, 0, 0, B - 1), (1, 1, 0, B - 1), (1, 0, B - 1, B), (1, 1, B - 1, B),
                   (1, 2, 0, B - 1), (1, 2, B - 1, B), (1, 3, 0, B - 1), (1, 3, B - 1, B)]

        def event(phase, t, whole):
            return 1 + max(n for n, (p, u, lo, hi) in enumerate(EVENTS) if (p, u) == (phase, t)
                           and (whole or lo == 0))

        def mm3(pe, res, a_hi, a_lo, b_hi, b_lo, start, stop):
            pe.matmul(res, a_hi, b_hi, start=start, stop=False)
            pe.matmul(res, a_hi, b_lo, start=False, stop=False)
            return pe.matmul(res, a_lo, b_hi, start=False, stop=stop)

        block = ctx.enter_context(nc.Block())

        @block.sync
        def _(sp):
            def row_of(src, f):
                return src[f].rearrange("(t p) d -> p t d", p=P)

            def chunk_load(src, t, rows):
                dst = xa if t % 2 == 0 else x1p
                sp.dma_start(dst[:, 0:rows], src[0:rows, t * P:(t + 1) * P, :].rearrange("b p d -> p b d")
                             ).then_inc(s_xr[t % 2], 16)

            def weight_load(t):
                sp.dma_start(route_w[:, t], switch_w[:, t]).then_inc(s_sw[t], 16)

            def table_loads():
                for n, (w, bias) in enumerate(((w1, b1), (w2, b2))):
                    sp.dma_start(tab[n][:, 0:HD, :], w.partition_broadcast(HPC)).then_inc(s_small, 16)
                    sp.dma_start(tab[n][:, HD, :], bias.partition_broadcast(HPC)).then_inc(s_small, 16)
                sp.dma_start(b3_half[:], b3.partition_broadcast(P)).then_inc(s_small, 16)
                sp.dma_start(sw_bias[:], switch_b.partition_broadcast(P)).then_inc(s_small, 16)

            for t in range(NT):
                if t >= 2:
                    sp.wait_ge(s_rn, event(0, t - 2, True))
                chunk_load(x, t, B)
                weight_load(t)
                if t == 1:
                    table_loads()
            sp.wait_ge(s_rn, event(0, 2, True))
            sp.dma_start(xa[:], row_of(x, 0)).then_inc(s_xa, 16)
            sp.dma_start(raw[:, 0, 0:KC * D].rearrange("p (k n) -> p k n", k=KC), w3).then_inc(s_raw[0], 16)
            sp.dma_start(raw[:, 1, 0:KC * D].rearrange("p (k n) -> p k n", k=KC), w_out).then_inc(s_raw[1], 16)
            sp.wait_ge(s_rn, event(0, 3, True))
            sp.dma_start(raw[:, 2, :], w_in[0]).then_inc(s_raw[2], 16)
            for g in range(1, KC):
                sp.wait_ge(s_wlo, g)
                sp.dma_start(raw[:, (g + 2) % 3, :], w_in[g]).then_inc(s_raw[2 + g], 16)

            def store_x2(b, t, src, job):
                sp.wait_ge(s_obf, job + 1)
                sp.dma_start(x2_dram[b, t * P:(t + 1) * P, :], src[:, t, :]).then_inc(s_x2, 16)

            with sp.Fori(0, B - 1) as b:
                sp.wait_ge(s_obf, b * len(ROW) + row_base)
                sp.dma_start(xa[:], row_of(x, b + 1)).then_inc(s_xa, 16)
                for t in range(NT):
                    store_x2(b, t, x1p, job_row(b, f"A{t}"))

            sp.wait_ge(s_x2, 16 * NT * (B - 1))
            sp.wait_ge(s_obf, last_base)
            chunk_load(x2_dram, 0, B - 1)
            chunk_load(x2_dram, 1, B - 1)
            sp.wait_ge(s_rn, event(1, 0, False))
            chunk_load(x2_dram, 2, B - 1)
            sp.wait_ge(s_rn, event(1, 1, False))
            chunk_load(x2_dram, 3, B - 1)
            sp.wait_ge(s_in, IN_JOBS * B)
            for t in range(NT - 1):
                weight_load(t)
            sp.wait_ge(s_y, KC * B)
            weight_load(NT - 1)
            for t in range(NT):
                store_x2(B - 1, t, x1, job_last(f"A{t}"))
            sp.wait_ge(s_rn, event(1, 2, False))
            sp.dma_start(xa[:], row_of(x2_dram, 0)).then_inc(s_xa, 16)
            sp.wait_ge(s_rm, 2 * NT)
            sp.dma_start(xa1[:], row_of(x2_dram, 1)).then_inc(s_xa1, 16)
            sp.dma_start(x1p[:], row_of(x2_dram, 2)).then_inc(s_xa2, 16)
            for f in range(B, 2 * B):
                for t in range(NT):
                    sp.wait_ge(s_obf, job_late(f, f"W{t}") + 1)
                    sp.dma_start(out[f - B, t * P:(t + 1) * P, :], x1[:, t, :]).then_inc(s_out[t], 16)
                if f == B:
                    sp.wait_ge(s_x2, 16 * NT * B)
                    sp.dma_start(xa[:], row_of(x2_dram, B - 1)).then_inc(s_xa, 16)
            for t in range(NT):
                sp.wait_ge(s_out[t], 16 * B)

        @block.tensor
        def _(pe):
            def route(phase):
                if phase == 1:
                    pe.wait_ge(s_obf, late_base - 1)
                for t in range(NT):
                    pe.wait_ge(s_sw[t], 16 * (phase + 1))
                    pe.wait_ge(s_rn, event(phase, t, True))
                    xn = xnw if t % 2 == 0 else xnr
                    for d in range(D // HD):
                        mm = pe.matmul(o_bank[0][:, 0:E * HD], xn[:, d * P:(d + 1) * P],
                                       route_w[:, t, :, d * HD:(d + 1) * HD],
                                       start=(t == 0 and d == 0), stop=(t == NT - 1 and d == D // HD - 1))
                    mm.then_inc(s_rm, 1)

            def logits(phase):
                if phase == 1:
                    pe.wait_ge(s_obf, late_base)
                pe.wait_ge(s_mix, phase + 1)
                pe.matmul(o_bank[1][:, 0:B * E], ones[:], lmix[:].rearrange("p b e -> p (b e)"),
                          start=True, stop=True).then_inc(s_lg, 1)

            def t1(f, after_row, after_ffn, meanwhile=lambda c: None):
                pe.wait_ge(s_xn, NT * (f + 1))
                for c in range(KC):
                    if c >= 2:
                        pe.wait_ge(s_t1e, KC * f + c - 1)
                    elif after_row is not None:
                        pe.wait_ge(s_mse if c == 0 else s_qn, KC * (after_row + 1))
                    elif after_ffn:
                        pe.wait_ge(s_t1e, KC * f)
                    for t in range(NT):
                        tp = pe.transpose(t_bank[c % 2][:, t * P:(t + 1) * P],
                                          xnw[:, t * D + c * P:t * D + (c + 1) * P], ident[:])
                    tp.then_inc(s_t1, 1)
                    meanwhile(c)

            def hidden(f, c, after_row, after_ffn):
                use = ffn_set(f)
                if c == 0:
                    pe.wait_ge(s_sel[0], f + 1)
                pe.wait_ge(s_t1e, KC * f + c + 1)
                pe.wait_ge(s_xtl, KC * f + c + 1)
                for k in range(TOPK):
                    j = TOPK * c + k
                    if j >= 4:
                        pe.wait_ge(s_gelu, H_JOBS * f + j - 3)
                    elif after_row is not None:
                        pe.wait_ge(s_ina, IN_JOBS * after_row + 17 + j)
                        if j == 2:
                            pe.wait_ge(s_u, KC * (after_row + 1))
                    elif after_ffn:
                        pe.wait_ge(s_gelu, H_JOBS * f - 3 + j)
                    mm3(pe, in_bank[j % 4][:], use["w_hi"][0][:, k, :], use["w_lo"][0][:, k, :],
                        xt_hi[:, c % 2, :], xt_lo[:, c % 2, :], True, True).then_inc(s_h, 1)

            def bank_free(job, first=False):
                if not first:
                    pe.wait_ge(s_obf, job - 1)

            def experts_out(f, c, job, first=False):
                use = ffn_set(f)
                if c == 0:
                    pe.wait_ge(s_sel[1], f + 1)
                bank_free(job, first)
                _, hi, lo = hid_set(f, c)
                bank = o_bank[job_bank(job)]
                for k in range(TOPK):
                    pe.wait_ge(s_hl, H_JOBS * f + TOPK * c + k + 1)
                    mm = mm3(pe, bank[:], use["w_hi"][1][:, k, :], use["w_lo"][1][:, k, :], hi[:, k, :],
                             lo[:, k, :], k == 0, k == TOPK - 1)
                mm.then_inc(s_ob, 1)

            def project(t, job, a_hi, a_lo, w_hi, w_lo, chunks=range(KC), chunk_wait=lambda k: None):
                if chunks[0] == 0:
                    bank_free(job)
                tok = slice(t * P, (t + 1) * P)
                bank = o_bank[job_bank(job)]
                for k in chunks:
                    chunk_wait(k)
                    mm = mm3(pe, bank[:], a_hi[:, k, tok], a_lo[:, k, tok], w_hi[:, k, :], w_lo[:, k, :],
                             k == 0, k == KC - 1)
                if chunks[-1] == KC - 1:
                    mm.then_inc(s_ob, 1)

            def w3_tile(f, t, job):
                use = ffn_set(f)

                def z_ready(k):
                    if t == 0:
                        pe.wait_ge(s_zh, KC * f + k + 1)
                        pe.wait_ge(s_zl, KC * f + k + 1)

                project(t, job, use["z_hi"], use["z_lo"], w3_hi, w3_lo, chunk_wait=z_ready)

            def out_tile(b, t, job, chunks=range(KC)):
                if t == 0:
                    pe.wait_ge(s_yh, KC * b + chunks[-1] + 1)
                    pe.wait_ge(s_yl, KC * b + chunks[-1] + 1)
                project(t, job, y_hi, y_lo, wo_hi, wo_lo, chunks)

            def t2(b, t):
                pe.wait_ge(s_xn1, NT * b + t + 1)
                if t >= 2:
                    pe.wait_ge(s_t2a, NT * b + t - 1)
                    pe.wait_ge(s_t2v, NT * b + t - 1)
                for c in range(KC):
                    tp = pe.transpose(t_bank[t % 2][:, c * P:(c + 1) * P],
                                      xnw[:, t * D + c * P:t * D + (c + 1) * P], ident[:])
                tp.then_inc(s_t2, 1)

            def in_part(b, first):
                pe.wait_ge(s_t2a, NT * (b + 1))
                pe.wait_ge(s_t2v, NT * (b + 1))
                for c in range(KC):
                    if first:
                        pe.wait_ge(s_whi, 3 + c)
                        if c < 2:
                            pe.wait_ge(s_wlo, 3 + c)
                        else:
                            pe.wait_ge(s_wlp, c - 1)
                    for r in range(ROLES):
                        j = ROLES * c + r
                        bank = in_bank[j % 4]
                        if j < 4:
                            pe.wait_ge(s_gelu, H_JOBS * b + 5 + j)
                        else:
                            pe.wait_ge(s_ina, IN_JOBS * b + j - 3)
                            if (j - 4) % ROLES == JOB_V:
                                pe.wait_ge(s_u, KC * b + (j - 4) // ROLES + 1)
                        for k in range(KC):
                            pe.matmul(bank[:], win_hi[:, c, r, k, :], xh[:, k, :], start=(k == 0), stop=False)
                            pe.matmul(bank[:], win_hi[:, c, r, k, :], xl[:, k, :], start=False, stop=False)
                        for k in range(KC):
                            mm = pe.matmul(bank[:], win_lo[:, c, r, k, :], xbf[:, k, :], start=False,
                                           stop=(k == KC - 1))
                        mm.then_inc(s_in, 1)
                        if r == JOB_A:
                            pe.wait_ge(s_sq, KC * b + c + 1)
                            if c >= 1:
                                pe.wait_ge(s_mse, KC * b + c)
                            for t in range(NT):
                                mm = pe.matmul(t_bank[0][:, t * HPC:(t + 1) * HPC], q_sq[:, t * P:(t + 1) * P],
                                               head_of[:], start=True, stop=True)
                            mm.then_inc(s_ms, 1)
                        if r == (JOB_V if c == KC - 1 else JOB_G):
                            pe.wait_ge(s_rsw, KC * b + c + 1)
                            if c >= 1:
                                pe.wait_ge(s_qn, KC * b + c)
                            for t in range(NT):
                                mm = pe.transpose(t_bank[1][:, t * P:(t + 1) * P],
                                                  rs_wide[:, t].rearrange("p j c -> p (j c)"), ident[:])
                            mm.then_inc(s_rst, 1)

            def job_bank(job):
                return job_parity[0]

            job_parity = [0]

            def run(parity, fn, *args, **part):
                job_parity[0] = parity % 2
                fn(*args, **part)

            def row_end(b):
                f = b + 1

                def do(name, **part):
                    job, parity = job_row(b, name), row_base + ROW.index(name)
                    n = int(name[1])
                    if name[0] == "O":
                        run(parity, experts_out, f, n, job)
                    elif name[0] == "W":
                        run(parity, w3_tile, f, n, job)
                    else:
                        run(parity, out_tile, b, n, job, **part)

                def meanwhile(c):
                    if c in (1, 2):
                        do(f"A{c - 1}", chunks=range(KC - 1))

                t1(f, b, False, meanwhile)
                hidden(f, 0, b, False)
                hidden(f, 1, b, False)
                for name in ("A0", "A1"):
                    do(name, chunks=range(KC - 1, KC))
                do("O0")
                hidden(f, 2, b, False)
                do("O1")
                hidden(f, 3, b, False)
                for name in ROW[ROW.index("O2"):]:
                    if name == "W3":
                        t2(f, 0)
                    if name == "A3":
                        t2(f, 1)
                        t2(f, 2)
                    do(name)
                t2(f, 3)

            pe.wait_ge(s_pc, 1)
            route(0)
            t1(0, None, False)
            logits(0)
            hidden(0, 0, None, False)
            hidden(0, 1, None, False)
            for c in range(KC):
                run(c, experts_out, 0, c, job_first(f"O{c}"), c < 2)
                if c < 2:
                    hidden(0, c + 2, None, False)
            pe.wait_ge(s_whi, 1)
            pe.wait_ge(s_wlo, 1)
            for t in range(NT):
                if t == 3:
                    t2(0, 0)
                run(t, w3_tile, 0, t, job_first(f"W{t}"))
            for t in range(1, NT):
                t2(0, t)
            in_part(0, True)
            row_end(0)
            with pe.Fori(1, B - 1) as b:
                in_part(b, False)
                row_end(b)
            in_part(B - 1, False)
            for chunks in (range(KC - 1), range(KC - 1, KC)):
                for t in range(2):
                    run(last_base + t, out_tile, B - 1, t, job_last(f"A{t}"), chunks)
            for t in range(2, NT):
                run(last_base + t, out_tile, B - 1, t, job_last(f"A{t}"))
            route(1)
            for f in range(B, 2 * B):
                after_row = B - 1 if f == B else None

                def filler(t):
                    if f > B:
                        job = job_late(f - 1, f"W{t}")
                        run(job, w3_tile, f - 1, t, job)

                t1(f, after_row, f > B)
                if f == B:
                    logits(1)
                hidden(f, 0, after_row, f > B)
                hidden(f, 1, after_row, f > B)
                for c in range(KC):
                    filler(c)
                    run(job_late(f, f"O{c}"), experts_out, f, c, job_late(f, f"O{c}"))
                    if c < 2:
                        hidden(f, c + 2, after_row, f > B)
            for t in range(NT):
                job = job_late(2 * B - 1, f"W{t}")
                run(job, w3_tile, 2 * B - 1, t, job)

        @block.scalar
        def _(act):
            def route_exp(phase):
                act.wait_ge(s_sh, phase + 1)
                act.activation(lg[:], lg[:], ACT.Exp).then_inc(s_exp, 1)

            def t1_out(f, c):
                act.wait_ge(s_t1, KC * f + c + 1)
                if c == 0 and not (isinstance(f, int) and f == 0):
                    act.wait_ge(s_zl, KC * f)
                if isinstance(f, int) and f > B and c < 2:
                    act.wait_ge(s_h, H_JOBS * (f - 1) + TOPK * (c + 3))
                act.activation(xt[:, c, :], t_bank[c % 2][:], ACT.Copy)
                act.activation(xt_hi[:, c % 2, :], t_bank[c % 2][:], ACT.Copy).then_inc(s_t1e, 1)

            def gelu(f, c):
                bufs = 1 if hid_set(f, 1) is hid0 else 2
                for k in range(TOPK):
                    act.wait_ge(s_h, H_JOBS * f + TOPK * c + k + 1)
                    if not (isinstance(f, int) and f == 0 and c == 0):
                        act.wait_ge(s_hl, H_JOBS * f + TOPK * (c - bufs) + k + 1)
                    act.activation(hid_set(f, c)[0][:, k, :], in_bank[(TOPK * c + k) % 4][:], ACT.Gelu,
                                   bias=ffn_set(f)["sel"][0][:, k, HD:FB]).then_inc(s_gelu, 1)

            def z_out(f, c, job):
                act.wait_ge(s_obf, job + 1)
                if isinstance(f, int) and f >= B + 2 and c == 0:
                    act.wait_ge(s_ob, job_late(f - 2, "W3") + 1)
                act.activation(ffn_set(f)["z_hi"][:, c, :], xt[:, c, :], ACT.Copy).then_inc(s_zh, 1)

            def ffn(f, job, begun=lambda: None, between=lambda n: None):
                t1_out(f, 0)
                t1_out(f, 1)
                begun()
                gelu(f, 0)
                t1_out(f, 2)
                gelu(f, 1)
                t1_out(f, 3)
                between(0)
                gelu(f, 2)
                z_out(f, 0, job("O0"))
                between(1)
                gelu(f, 3)
                for c in range(1, KC):
                    z_out(f, c, job(f"O{c}"))

            def t2_out(b):
                for t in range(NT):
                    act.wait_ge(s_t2, NT * b + t + 1)
                    src = t_bank[t % 2][:].rearrange("p (c s) -> p c s", c=KC)
                    cols = slice(t * P, (t + 1) * P)
                    act.activation(xh[:, :, cols], src, ACT.Copy)
                    act.activation(xbf[:, :, cols], src, ACT.Copy).then_inc(s_t2a, 1)

            def y_out(b, c):
                act.wait_ge(s_y, KC * b + c + 1)
                act.activation(y_hi[:, c, :], yt[:], ACT.Copy).then_inc(s_yh, 1)

            def group(b, c):
                def bank(r):
                    act.wait_ge(s_in, IN_JOBS * b + ROLES * c + r + 1)
                    return in_bank[(ROLES * c + r) % 4][:]

                src = bank(JOB_Q)
                if c >= 1:
                    act.wait_ge(s_ms, KC * b + c)
                act.activation(q_sq[:], src, ACT.Square).then_inc(s_sq, 1)
                if c >= 1:
                    act.wait_ge(s_qm, KC * b + c)
                act.activation(qt[:], src, ACT.Copy).then_inc(s_ina, 1)
                src = bank(JOB_A)
                act.activation(decay[:], src, ACT.Sigmoid, bias=two[:]).then_inc(s_ina, 1)
                act.wait_ge(s_ms, KC * b + c + 1)
                if c >= 1:
                    act.wait_ge(s_rs, KC * b + c)
                act.activation(ms[:], t_bank[0][:, 0:NT * HPC], ACT.Identity, scale=1.0 / HD,
                               bias=rms_eps[:]).then_inc(s_mse, 1)
                src = bank(JOB_K)
                act.activation(kt[:], src, ACT.Tanh).then_inc(s_ina, 1)
                src = bank(JOB_V)
                if c >= 1:
                    act.wait_ge(s_y, KC * b + c)
                    y_out(b, c - 1)
                act.activation(vt[:], src, ACT.Copy).then_inc(s_ina, 1)
                src = bank(JOB_G)
                act.activation(gt[:], src, ACT.Sigmoid).then_inc(s_ina, 1)

            def attention(b):
                for c in range(KC):
                    group(b, c)

            def split_hi(i, dst, src, scale=1.0):
                act.wait_ge(s_raw[i], 16)
                act.activation(dst, src, ACT.Copy, scale=scale).then_inc(s_whi, 1)

            def split_in(g):
                split_hi(2 + g, win_hi[:, g].rearrange("p r k n -> p (r k n)"), raw[:, (g + 2) % 3, :])

            def first_splits(n):
                if n == 0:
                    split_hi(1, wo_hi[:].rearrange("p k n -> p (k n)"), raw[:, 1, 0:KC * D])
                else:
                    split_in(0)

            def begun():
                split_hi(0, w3_hi[:].rearrange("p k n -> p (k n)"), raw[:, 0, 0:KC * D], 0.5)
                route_exp(0)

            act.wait_ge(s_pc, 1)
            ffn(0, job_first, begun, first_splits)
            split_in(1)
            split_in(2)
            t2_out(0)
            split_in(3)
            act.wait_ge(s_wlp, 2)
            with act.Fori(0, B - 1) as b:
                attention(b)
                ffn(b + 1, lambda name: job_row(b, name), lambda: y_out(b, KC - 1))
                t2_out(b + 1)
            attention(B - 1)
            y_out(B - 1, KC - 1)
            for f in range(B, 2 * B):
                ffn(f, lambda name: job_late(f, name), (lambda: route_exp(1)) if f == B else (lambda: None))

        @block.gpsimd
        def _(pool):
            own = Steps(pool, s_po)
            for ap, value in ((ident, 0.0), (diag, 0.0), (head_of, 1.0), (neg_half, -0.5), (two, 2.0), (ones, 1.0),
                              (rms_eps, RMS_EPS)):
                own.mark(pool.memset(ap[:], value))
            for e in range(E):
                own.mark(pool.memset(rank[:, e:e + 1], float(E - e)))
            own.wait(own.n)
            own.mark(pool.affine_select(out=ident[:], in_=ident[:], compare_op=ALU.not_equal, fill=1.0, base=0,
                                        pattern=[[-1, P]], channel_multiplier=1))
            for j in range(HPC):
                own.do(pool.affine_select(out=diag[:], in_=diag[:], compare_op=ALU.not_equal, fill=1.0,
                                          base=-HD * j, pattern=[[-1, HD]], channel_multiplier=1))
            own.do(pool.affine_select(out=head_of[:], in_=head_of[:], compare_op=ALU.is_ge, fill=0.0, base=0,
                                      pattern=[[-HD, HPC]], channel_multiplier=1))
            pool.affine_select(out=head_of[:], in_=head_of[:], compare_op=ALU.is_ge, fill=0.0, base=HD - 1,
                               pattern=[[HD, HPC]], channel_multiplier=-1).then_inc(s_pc, 1)

            def route_rstd(n):
                _, t, lo, hi = EVENTS[n]
                pool.wait_ge(s_rv, n + 1)
                pool.tensor_tensor(rstd[:, lo:hi, t], mv[:, lo:hi, t, 1], neg_half[:, 0:hi - lo],
                                   ALU.pow).then_inc(s_rp, 1)

            def xt_split(f, c):
                pool.wait_ge(s_t1e, KC * f + c + 1)
                if c >= 2:
                    pool.wait_ge(s_h, H_JOBS * f + TOPK * (c - 1))
                pool.tensor_tensor(xt_lo[:, c % 2, :], xt[:, c, :], xt_hi[:, c % 2, :],
                                   ALU.subtract).then_inc(s_xtl, 1)

            def z_split(f, c):
                use = ffn_set(f)
                pool.wait_ge(s_zh, KC * f + c + 1)
                pool.tensor_tensor(use["z_lo"][:, c, :], xt[:, c, :], use["z_hi"][:, c, :],
                                   ALU.subtract).then_inc(s_zl, 1)

            def residual_bias(f, t):
                ap = ffn_input(f)[0][:, t, :]
                pool.wait_ge(s_xn, NT * f + t + 1)
                pool.tensor_tensor(ap, ap, b3_half[:], ALU.add).then_inc(s_xb, 1)

            def ffn(f):
                for c in range(KC):
                    xt_split(f, c)
                for c in range(KC):
                    z_split(f, c)

            def ln_rstd(b):
                for t in range(NT):
                    pool.wait_ge(s_v1, NT * b + t + 1)
                    pool.tensor_tensor(rstd1[:, t:t + 1], mv1[:, t, 1:2], neg_half[:, 0:1],
                                       ALU.pow).then_inc(s_p1, 1)

            def group(b, c):
                pool.wait_ge(s_mse, KC * b + c + 1)
                if c >= 1:
                    pool.wait_ge(s_rsw, KC * b + c)
                pool.tensor_tensor(rs[:], ms[:], neg_half[:], ALU.pow).then_inc(s_rs, 1)
                pool.wait_ge(s_rs, KC * b + c + 1)
                if c >= 1:
                    pool.wait_ge(s_rst, KC * b + c)
                pool.tensor_tensor(rs_wide[:].rearrange("p t j c -> p (t j) c"),
                                   rs[:].unsqueeze(2).to_broadcast([P, NT * HPC, HD]),
                                   ones[:, 0:1].unsqueeze(2).to_broadcast([P, NT * HPC, HD]),
                                   ALU.mult).then_inc(s_rsw, 1)
                pool.wait_ge(s_ina, IN_JOBS * b + ROLES * c + JOB_G + 1)
                pool.tensor_tensor(gv[:], gt[:], vt[:], ALU.mult).then_inc(s_gv, 1)
                pool.wait_ge(s_gv, KC * b + c + 1)
                pool.tensor_tensor(vt[:], vt[:], gv[:], ALU.subtract).then_inc(s_w, 1)

            for n in range(NT):
                route_rstd(n)
            pool.wait_ge(s_vc, 1)
            for t in range(NT):
                residual_bias(0, t)
            ffn(0)
            ln_rstd(0)
            for g in (2, 3):
                pool.wait_ge(s_whi, 3 + g)
                pool.tensor_tensor(win_lo[:, g].rearrange("p r k n -> p (r k n)"), raw[:, (g + 2) % 3, :],
                                   win_hi[:, g].rearrange("p r k n -> p (r k n)"), ALU.subtract).then_inc(s_wlp, 1)
            with pool.Fori(0, B - 1) as b:
                for c in range(KC):
                    group(b, c)
                    if c == 2:
                        for t in range(NT):
                            residual_bias(b + 1, t)
                ffn(b + 1)
                ln_rstd(b + 1)
            for c in range(KC):
                group(B - 1, c)
                if c in (1, 2):
                    route_rstd(NT + c - 1)
            for n in range(NT + 2, len(EVENTS)):
                route_rstd(n)
            for f in range(B, 2 * B):
                for c in range(KC):
                    xt_split(f, c)
                for c in range(KC):
                    z_split(f, c)
                    residual_bias(f, c)

        @block.vector
        def _(ve):
            own = Steps(ve, s_ve)

            def route_event(n):
                phase, t, lo, hi = EVENTS[n]
                slot = xa if t % 2 == 0 else x1p
                xn = xnw if t % 2 == 0 else xnr
                if lo == 0:
                    ve.wait_ge(s_xr[t % 2], 16 * (2 * phase + t // 2 + 1))

                def src(b):
                    return x1[:, t, :] if lo > 0 else slot[:, b, :]

                for b in range(lo, hi):
                    m = own.mark(ve.bn_stats(stats[:, b, :], src(b)))
                own.wait(m)
                for b in range(lo, hi):
                    m = own.mark(ve.bn_aggr(mv[:, b, t, :], stats[:, b, :]))
                own.wait(m)
                ve.tensor_scalar(mv[:, lo:hi, t, 1], mv[:, lo:hi, t, 1], LN_EPS, None, ALU.add).then_inc(s_rv, 1)
                ve.wait_ge(s_rp, n + 1)
                if t >= 2:
                    ve.wait_ge(s_rm, NT * phase + t - 1)
                for b in range(lo, hi):
                    dst = xn[:].rearrange("p (d b c) -> p d b c", b=B, c=HD)[:, :, b, :]
                    ins = ve.tensor_scalar(dst, src(b).rearrange("p (d c) -> p d c", c=HD),
                                           mv[:, b, t, 0:1], rstd[:, b, t:t + 1], ALU.subtract, ALU.mult)
                ins.then_inc(s_rn, 1)

            def choose(phase):
                def over_e(ap):
                    return ap.unsqueeze(2).to_broadcast([P, B, E])

                ve.wait_ge(s_rm, NT * (phase + 1))
                acc = o_bank[0][:, 0:E * HD].rearrange("p (e c) -> p e c", e=E)
                scratch = prod[:].rearrange("p k f e -> p (k f e)")[:, 0:E * HD].rearrange("p (e c) -> p e c", e=E)
                own.do(ve.tensor_tensor(scratch, acc, diag[:].unsqueeze(1).to_broadcast([P, E, HD]), ALU.mult))
                own.do(ve.tensor_reduce(part[:], scratch, AX.X, ALU.add))
                ve.tensor_tensor(lmix[:], part[:].unsqueeze(1).to_broadcast([P, B, E]), over_e(head_of[:]),
                                 ALU.mult).then_inc(s_mix, 1)
                ve.wait_ge(s_lg, phase + 1)
                own.do(ve.tensor_tensor(lg[:], o_bank[1][:, 0:B * E].rearrange("p (b e) -> p b e", b=B),
                                        sw_bias[:].unsqueeze(1).to_broadcast([P, B, E]), ALU.add))
                own.do(ve.tensor_reduce(red[:], lg[:], AX.X, ALU.max))
                ve.tensor_tensor(lg[:], lg[:], over_e(red[:]), ALU.subtract).then_inc(s_sh, 1)
                ve.wait_ge(s_exp, phase + 1)
                own.do(ve.tensor_reduce(red[:], lg[:], AX.X, ALU.add))
                own.do(ve.reciprocal(red2[:], red[:]))
                own.do(ve.tensor_tensor(lg[:], lg[:], over_e(red2[:]), ALU.mult))
                for k in range(TOPK):
                    own.do(ve.tensor_reduce(gates[:, :, k], lg[:], AX.X, ALU.max))
                    own.do(ve.tensor_tensor(eq[:], lg[:], over_e(gates[:, :, k]), ALU.is_equal))
                    own.do(ve.tensor_tensor(eq[:], eq[:], rank[:].unsqueeze(1).to_broadcast([P, B, E]), ALU.mult))
                    own.do(ve.tensor_reduce(red[:], eq[:], AX.X, ALU.max))
                    own.do(ve.tensor_tensor(pick[:, :, k, :], eq[:], over_e(red[:]), ALU.is_equal))
                    m = own.mark(ve.tensor_tensor(pick_g[:, :, k, :], pick[:, :, k, :], over_e(gates[:, :, k]),
                                                  ALU.mult))
                    if k == 0:
                        m = own.mark(ve.scalar_tensor_tensor(out=lg[:], in0=pick[:, :, 0, :], scalar=-2.0,
                                                             in1=lg[:], op0=ALU.mult, op1=ALU.add))
                    own.wait(m)

            def select(row, f):
                use = ffn_set(f)
                for n, choice in enumerate((pick, pick_g)):
                    sel, hi, lo = use["sel"][n], use["w_hi"][n], use["w_lo"][n]
                    for k in range(TOPK):
                        m = own.mark(ve.tensor_tensor(
                            prod[:, k], tab[n][:],
                            choice[:, bass.ds(row, 1), k, :].to_broadcast([P, FB, E]), ALU.mult))
                    own.wait(m)
                    own.do(ve.tensor_reduce(sel[:], prod[:], AX.X, ALU.add))
                    for k in range(TOPK):
                        m = own.mark(ve.tensor_tensor(
                            w_diag[:, k], sel[:, k, 0:HD].unsqueeze(1).to_broadcast([P, HPC, HD]),
                            head_of[:].unsqueeze(2).to_broadcast([P, HPC, HD]), ALU.mult))
                    if n == 1:
                        m = own.mark(ve.tensor_tensor(use["b2"][:], sel[:, 0, HD:FB], sel[:, 1, HD:FB], ALU.add))
                    own.wait(m)
                    own.do(ve.tensor_copy(hi[:].rearrange("p k (j c) -> p k j c", j=HPC), w_diag[:]))
                    ve.tensor_tensor(lo[:].rearrange("p k (j c) -> p k j c", j=HPC), w_diag[:],
                                     hi[:].rearrange("p k (j c) -> p k j c", j=HPC),
                                     ALU.subtract).then_inc(s_sel[n], 1)
                    ve.wait_ge(s_sel[n], f + 1)

            def normalise(f, row):
                src, *loaded = ffn_input(f)
                ve.wait_ge(*loaded)
                for t in range(NT):
                    ve.tensor_scalar(xnw[:, t * D:(t + 1) * D], src[:, t, :], mv[:, bass.ds(row, 1), t, 0],
                                     rstd[:, bass.ds(row, 1), t], ALU.subtract, ALU.mult).then_inc(s_xn, 1)

            def split_hidden(f, c, read_job):
                src, hi, lo = hid_set(f, c)
                for k in range(TOPK):
                    ve.wait_ge(s_gelu, H_JOBS * f + TOPK * c + k + 1)
                    if k == 0 and read_job is not None:
                        ve.wait_ge(s_ob, read_job + 1)
                    own.do(ve.tensor_copy(hi[:, k, :], src[:, k, :]))
                    ve.tensor_tensor(lo[:, k, :], src[:, k, :], hi[:, k, :], ALU.subtract).then_inc(s_hl, 1)

            def add_experts(f, c, job, parity):
                ve.wait_ge(s_ob, job + 1)
                ve.scalar_tensor_tensor(out=xt[:, c, :], in0=o_bank[parity % 2][:], scalar=ffn_set(f)["b2"][:],
                                        in1=xt[:, c, :], op0=ALU.add, op1=ALU.add).then_inc(s_obf, 1)

            def w3_add(f, t, job, parity):
                ve.wait_ge(s_xb, NT * f + t + 1)
                ve.wait_ge(s_ob, job + 1)
                ve.tensor_tensor(x1[:, t, :], o_bank[parity % 2][:], ffn_input(f)[0][:, t, :],
                                 ALU.add).then_inc(s_obf, 1)

            def norm1(f, t):
                ve.wait_ge(s_p1, NT * f + t + 1)
                ve.tensor_scalar(xnw[:, t * D:(t + 1) * D], x1[:, t, :], mv1[:, t, 0:1], rstd1[:, t:t + 1],
                                 ALU.subtract, ALU.mult).then_inc(s_xn1, 1)

            def w3_norm(f, t, job, parity):
                if t >= 1:
                    norm1(f, t - 1)
                w3_add(f, t, job, parity)
                ve.wait_ge(s_obf, job + 1)
                own.do(ve.bn_stats(stats[:, t, :], x1[:, t, :]))
                ve.tensor_copy(fence[:], neg_half[:, 0:1])
                own.do(ve.bn_aggr(mv1[:, t, :], stats[:, t, :]))
                ve.tensor_scalar(mv1[:, t, 1:2], mv1[:, t, 1:2], LN_EPS, None, ALU.add).then_inc(s_v1, 1)
                if t == NT - 1:
                    norm1(f, t)

            def out_add(t, job, parity, src, dst):
                ve.wait_ge(s_ob, job + 1)
                ve.tensor_tensor(dst[:, t, :], src[:, t, :], o_bank[parity % 2][:], ALU.add).then_inc(s_obf, 1)

            def t2_lo(b, t):
                ve.wait_ge(s_t2a, NT * b + t + 1)
                cols = slice(t * P, (t + 1) * P)
                ve.tensor_tensor(xl[:, :, cols], t_bank[t % 2][:].rearrange("p (c s) -> p c s", c=KC),
                                 xh[:, :, cols], ALU.subtract).then_inc(s_t2v, 1)

            def group(b, c):
                job = IN_JOBS * b + ROLES * c
                ve.wait_ge(s_ina, job + JOB_A + 1)
                own.do(ve.tensor_scalar(decay[:], decay[:], A_MIN, A_MAX, ALU.max, ALU.min))
                first = decay[:].rearrange("p (n s) -> p n s", s=CHUNK)[:, :, 0:1]
                own.do(ve.tensor_scalar(starts[:].rearrange("p (n s) -> p n s", s=CHUNK)[:, :, 0:1], first,
                                        1.0 / GUARD, None, ALU.mult))
                pref_done = own.mark(ve.tensor_tensor_scan(pref[:], decay[:], starts[:], 0.0, ALU.mult, ALU.max))
                ve.wait_ge(s_ina, job + JOB_V + 1)
                ve.tensor_tensor(kt[:], kt[:], in_bank[(ROLES * c + JOB_V) % 4][:], ALU.mult).then_inc(s_u, 1)
                ve.wait_ge(s_u, KC * b + c + 1)
                own.wait(pref_done)
                in_done = own.mark(ve.scalar_tensor_tensor(out=pref[:], in0=pref[:], scalar=1.0, in1=kt[:],
                                                           op0=ALU.min, op1=ALU.mult))
                ve.wait_ge(s_rst, KC * b + c + 1)
                ve.tensor_tensor(qt[:], qt[:], t_bank[1][:], ALU.mult).then_inc(s_qn, 1)
                own.wait(in_done)
                own.do(ve.tensor_tensor_scan(kt[:], decay[:], pref[:], 0.0, ALU.mult, ALU.add))
                ve.wait_ge(s_qn, KC * b + c + 1)
                ve.tensor_tensor(yt[:], qt[:], kt[:], ALU.mult).then_inc(s_qm, 1)
                ve.wait_ge(s_qm, KC * b + c + 1)
                ve.wait_ge(s_ina, job + JOB_G + 1)
                own.do(ve.tensor_tensor(yt[:], yt[:], gt[:], ALU.mult))
                ve.wait_ge(s_w, KC * b + c + 1)
                ve.tensor_tensor(yt[:], yt[:], vt[:], ALU.add).then_inc(s_y, 1)

            def y_low(b, c):
                ve.wait_ge(s_yh, KC * b + c + 1)
                ve.tensor_tensor(y_lo[:, c, :], yt[:], y_hi[:, c, :], ALU.subtract).then_inc(s_yl, 1)

            def split_lo(i, dst, src, hi, scale=None):
                ve.wait_ge(s_whi, i + 1)
                if scale is None:
                    ins = ve.tensor_tensor(dst, src, hi, ALU.subtract)
                else:
                    ins = ve.scalar_tensor_tensor(out=dst, in0=src, scalar=scale, in1=hi, op0=ALU.mult,
                                                  op1=ALU.subtract)
                ins.then_inc(s_wlo, 1)

            def split_in(g):
                split_lo(2 + g, win_lo[:, g].rearrange("p r k n -> p (r k n)"), raw[:, (g + 2) % 3, :],
                         win_hi[:, g].rearrange("p r k n -> p (r k n)"))

            def attention(b, before):
                for c in range(KC):
                    group(b, c)
                    before(c)
                    y_low(b, c)

            ve.wait_ge(s_pc, 1)
            for n in range(NT):
                route_event(n)
            ve.wait_ge(s_rm, NT - 1)
            normalise(0, 0)
            ve.wait_ge(s_small, 16 * 6)
            ve.tensor_scalar(b3_half[:], b3_half[:], 0.5, None, ALU.mult).then_inc(s_vc, 1)
            choose(0)
            select(0, 0)
            split_hidden(0, 0, None)
            for c in range(KC):
                if c < KC - 1:
                    split_hidden(0, c + 1, job_first(f"O{c}"))
                add_experts(0, c, job_first(f"O{c}"), c)
                if c == 0:
                    split_lo(0, w3_lo[:].rearrange("p k n -> p (k n)"), raw[:, 0, 0:KC * D],
                             w3_hi[:].rearrange("p k n -> p (k n)"), 0.5)
                if c == 1:
                    split_lo(1, wo_lo[:].rearrange("p k n -> p (k n)"), raw[:, 1, 0:KC * D],
                             wo_hi[:].rearrange("p k n -> p (k n)"))
            split_in(0)
            for t in range(NT):
                if t == 2:
                    own.do(ve.memset(starts[:], 0.0))
                w3_norm(0, t, job_first(f"W{t}"), t)
                if t >= 2:
                    t2_lo(0, t - 2)
            split_in(1)
            t2_lo(0, 2)
            t2_lo(0, 3)

            base = own.base + own.n
            with ve.Fori(0, B - 1) as b:
                own.base, own.n = base + b * VE_ROW_STEPS, 0

                def before(c):
                    if c == 0:
                        select(b + 1, b + 1)
                    if c == 1:
                        normalise(b + 1, b + 1)

                attention(b, before)
                split_hidden(b + 1, 0, None)
                for name in ROW:
                    job, parity, n = job_row(b, name), row_base + ROW.index(name), int(name[1])
                    if name[0] == "O":
                        if n < KC - 1:
                            split_hidden(b + 1, n + 1, job)
                        add_experts(b + 1, n, job, parity)
                    elif name[0] == "W":
                        if n == NT - 1:
                            t2_lo(b + 1, 0)
                            own.do(ve.tensor_copy(x1p[:, n, :], x1[:, n, :]))
                        w3_norm(b + 1, n, job, parity)
                    elif n < NT - 1:
                        out_add(n, job, parity, x1, x1p)
                    else:
                        for t in range(1, NT):
                            t2_lo(b + 1, t)
                        out_add(n, job, parity, x1p, x1p)
                assert own.n == VE_ROW_STEPS, own.n

            own.base, own.n = base + (B - 1) * VE_ROW_STEPS, 0

            def early(c):
                if c in (1, 2):
                    route_event(NT + c - 1)

            attention(B - 1, early)
            for t in range(NT):
                out_add(t, job_last(f"A{t}"), last_base + t, x1, x1)
                if t < 2:
                    ve.wait_ge(s_obf, job_last(f"A{t}") + 1)
                    route_event(NT + 2 + t)
            ve.wait_ge(s_obf, late_base)
            for n in range(NT + 4, len(EVENTS)):
                route_event(n)
            ve.wait_ge(s_rm, 2 * NT - 1)
            normalise(B, 0)
            choose(1)
            select(0, B)
            for f in range(B, 2 * B):
                split_hidden(f, 0, None)
                for c in range(KC):
                    if f > B:
                        job = job_late(f - 1, f"W{c}")
                        if f > B + 1:
                            ve.wait_ge(s_out[c], 16 * (f - B - 1))
                        elif c == 0:
                            ve.wait_ge(s_x2, 16 * NT * B)
                        w3_add(f - 1, c, job, job)
                    if c < KC - 1:
                        split_hidden(f, c + 1, job_late(f, f"O{c - 1}") if c >= 1 else None)
                    add_experts(f, c, job_late(f, f"O{c}"), job_late(f, f"O{c}"))
                    if f + 1 < 2 * B:
                        if c == 0:
                            ve.wait_ge(s_rm, 2 * NT)
                            select(f + 1 - B, f + 1)
                        if c == 2:
                            ve.wait_ge(s_t1, KC * (f + 1))
                            normalise(f + 1, f + 1 - B)
            for t in range(NT):
                job = job_late(2 * B - 1, f"W{t}")
                ve.wait_ge(s_out[t], 16 * (B - 1))
                w3_add(2 * B - 1, t, job, job)


VE_ROW_STEPS = 54


def kernel(**inputs):
    import numpy as np
    import concourse.bacc as bacc
    from concourse.bass_utils import run_bass_kernel_spmd

    a = {k.replace("L0_attn_", "").replace("L0_ffn_", ""): np.asarray(v) for k, v in inputs.items()}
    w_in = a["w_in"].reshape(5, KC, P, KC, P)[[0, 3, 1, 2, 4]].transpose(1, 4, 0, 3, 2)
    arrays = {
        "x": a["x"],
        "w_in": w_in.reshape(KC, P, ROLES * KC * P),
        "w_out": a["w_out"].T.reshape(KC, P, D).transpose(1, 0, 2),
        "switch_w": a["switch_w"].reshape(E, NT, P, D).transpose(2, 1, 0, 3),
        "switch_b": a["switch_b"],
        "w1": a["w1"].transpose(2, 1, 0),
        "b1": a["b1"].T,
        "w2": a["w2"].transpose(2, 1, 0),
        "b2": a["b2"].T,
        "w3": a["w3"].T.reshape(KC, P, D).transpose(1, 0, 2),
        "b3": a["b3"],
    }
    nc = bacc.Bacc("TRN2", target_bir_lowering=False, num_devices=1)
    feed, args = {}, []
    for name, arr in arrays.items():
        arr = np.ascontiguousarray(arr)
        feed[f"in_{name}"] = arr
        args.append(nc.dram_tensor(f"in_{name}", arr.shape, mybir.dt.from_np(arr.dtype), kind="ExternalInput").ap())
    args.append(nc.dram_tensor("out_0", (B, S, D), F32, kind="ExternalOutput").ap())
    macaron_kernel(nc, *args)
    r = run_bass_kernel_spmd(nc, [feed], core_ids=[0])
    return r.results[0]["out_0"]
```

```python
from contextlib import ExitStack

import concourse.bass as bass
from concourse import mybir

P = 128
ALU = mybir.AluOpType
ACT = mybir.ActivationFunctionType
AX = mybir.AxisListType
F32 = mybir.dt.float32
F32R = mybir.dt.float32r
BF16 = mybir.dt.bfloat16

B, S, D = 4, 512, 512
NT = S // P
KC = D // P
E, TOPK = 8, 2
HD = 32
HPC = P // HD
CHUNK = 64
ROLES = 5
GUARD = 1e-6
LN_EPS = 1e-5
RMS_EPS = 1.1920928955078125e-07
A_MIN, A_MAX = 0.6, 0.9995
TAKEN = -3e38
FB = HD + 1


JOB_Q, JOB_A, JOB_K, JOB_V, JOB_G = range(ROLES)
IN_JOBS = ROLES * KC
H_JOBS = TOPK * KC


class Steps:

    def __init__(self, eng, sem):
        self.eng, self.sem, self.base, self.n = eng, sem, 0, 0

    def mark(self, ins):
        self.n += 1
        ins.then_inc(self.sem, 1)
        return self.base + self.n

    def wait(self, value):
        self.eng.wait_ge(self.sem, value)

    def do(self, ins):
        self.wait(self.mark(ins))


def macaron_kernel(nc, x, w_in, w_out, switch_w, switch_b, w1, b1, w2, b2, w3, b3, out):
    x2_dram = nc.dram_tensor("x2_dram", (B, S, D), F32).ap()

    with ExitStack() as ctx:
        def sb(name, shape, dt=F32, into=ctx):
            return into.enter_context(nc.sbuf_tensor(name, shape, dt))

        def sem(name):
            return ctx.enter_context(nc.semaphore(name))

        with ExitStack() as region:
            route_w = sb("route_w", [P, NT, D // HD, E, HD], into=region)
        with ExitStack() as region:
            z_hi1 = sb("z_hi1", [P, KC, S], F32R, into=region)
            z_lo1 = sb("z_lo1", [P, KC, S], F32R, into=region)
            xa1 = sb("xa1", [P, NT, D], into=region)
            xt1 = sb("xt1", [P, KC, S], into=region)
            xt_hi1 = sb("xt_hi1", [P, KC, S], F32R, into=region)
            xt_lo1 = sb("xt_lo1", [P, KC, S], F32R, into=region)
            hf1 = sb("hf1", [P, TOPK, S], into=region)
            h_hi1 = sb("h_hi1", [P, TOPK, S], F32R, into=region)
            h_lo1 = sb("h_lo1", [P, TOPK, S], F32R, into=region)
        win_hi = sb("win_hi", [P, KC, ROLES, KC, P], F32R)
        win_lo = sb("win_lo", [P, KC, ROLES, KC, P], BF16)
        gt = sb("gt", [P, S])
        starts = sb("starts", [P, S])

        w3_hi = sb("w3_hi", [P, KC, D], F32R)
        w3_lo = sb("w3_lo", [P, KC, D], F32R)
        wo_hi = sb("wo_hi", [P, KC, D], F32R)
        wo_lo = sb("wo_lo", [P, KC, D], F32R)
        xa = sb("xa", [P, NT, D])
        x1 = sb("x1", [P, NT, D])
        xnw = sb("xnw", [P, NT * D])
        with ExitStack() as region:
            xnr = sb("xnr", [P, NT * D], into=region)
        z_lo = sb("z_lo", [P, KC, S], F32R)

        with ExitStack() as region:
            xh = sb("xh", [P, KC, S], F32R, into=region)
            xl = sb("xl", [P, KC, S], F32R, into=region)
            xbf = sb("xbf", [P, KC, S], BF16, into=region)
            prod = sb("prod", [P, TOPK, FB, E], into=region)
            w_diag = sb("w_diag", [P, TOPK, HPC, HD], into=region)
            gv = sb("gv", [P, S], into=region)
            sb("r1_pad", [P, 2048 - TOPK * FB * E - TOPK * P - S], into=region)
            pref = sb("pref", [P, S], into=region)
            kt = sb("kt", [P, S], into=region)
            vt = sb("vt", [P, S], into=region)
            rs_wide = sb("rs_wide", [P, NT, HPC, HD], into=region)
        xt = sb("xt", [P, KC, S])
        xt_hi = sb("xt_hi", [P, 2, S], F32R)
        xt_lo = sb("xt_lo", [P, 2, S], F32R)
        hf = sb("hf", [P, TOPK, S])
        h_hi = sb("h_hi", [P, TOPK, S], F32R)
        h_lo = sb("h_lo", [P, TOPK, S], F32R)
        z_hi = sb("z_hi", [P, KC, S], F32R)

        with ExitStack() as region:
            raw = sb("raw", [P, 3, ROLES * KC * P], into=region)
        with ExitStack() as region:
            xt_hi_late = sb("xt_hi_late", [P, KC, S], F32R, into=region)
            xt_lo_late = sb("xt_lo_late", [P, KC, S], F32R, into=region)
            sel1 = [sb(n, [P, TOPK, FB], into=region) for n in ("w1_sel1", "w2_sel1")]
            w_hi1 = [sb(n, [P, TOPK, P], F32R, into=region) for n in ("w1_hi1", "w2_hi1")]
            w_lo1 = [sb(n, [P, TOPK, P], F32R, into=region) for n in ("w1_lo1", "w2_lo1")]
            b2_col1 = sb("b2_col1", [P, 1], into=region)
            prod_late = sb("prod_late", [P, TOPK, FB, E], into=region)
            w_diag_late = sb("w_diag_late", [P, TOPK, HPC, HD], into=region)
        y_hi = sb("y_hi", [P, KC, S], F32R)
        y_lo = sb("y_lo", [P, KC, S], F32R)
        decay = sb("decay", [P, S])
        qt = sb("qt", [P, S])
        q_sq = sb("q_sq", [P, S])
        yt = sb("yt", [P, S])
        x1p = sb("x1p", [P, NT, D])

        ident = sb("ident", [P, P])
        ones = sb("ones", [P, P])
        head_of = sb("head_of", [P, HPC])
        diag = sb("diag", [P, HD])
        tab = [sb(n, [P, FB, E]) for n in ("w1_tab", "w2_tab")]
        sel0 = [sb(n, [P, TOPK, FB]) for n in ("w1_sel", "w2_sel")]
        w_hi0 = [sb(n, [P, TOPK, P], F32R) for n in ("w1_hi", "w2_hi")]
        w_lo0 = [sb(n, [P, TOPK, P], F32R) for n in ("w1_lo", "w2_lo")]
        b2_col0 = sb("b2_col", [P, 1])
        b3_half = sb("b3_half", [P, D])
        sw_bias = sb("sw_bias", [P, E])
        stats = sb("stats", [P, NT, 6])
        mv = sb("mv", [P, B, NT, 2])
        rstd = sb("rstd", [P, B, NT])
        mv1 = sb("mv1", [P, NT, 2])
        rstd1 = sb("rstd1", [P, NT])
        neg_half = sb("neg_half", [P, NT * HPC])
        ms = sb("ms", [P, NT * HPC])
        rs = sb("rs", [P, NT * HPC])
        two = sb("two", [P, 1])
        rms_eps = sb("rms_eps", [P, 1])
        table_out = sb("table_out", [P, 1])
        part = sb("part", [P, E])
        lmix = sb("lmix", [P, B, E])
        lg = sb("lg", [P, B, E])
        lg2 = sb("lg2", [P, B, E])
        probs = sb("probs", [P, B, E])
        eq = sb("eq", [P, B, E])
        rank = sb("rank", [P, E])
        red = sb("red", [P, B])
        fence = sb("fence", [P, 1])
        pick = sb("pick", [P, B, TOPK, E])
        pick_g = sb("pick_g", [P, B, TOPK, E])

        ffn0 = dict(z_hi=z_hi, z_lo=z_lo, sel=sel0, w_hi=w_hi0, w_lo=w_lo0, b2=b2_col0, xt=xt, xt_hi=xt_hi,
                    xt_lo=xt_lo, prod=prod, w_diag=w_diag)
        late0 = dict(ffn0, xt_hi=xt_hi_late, xt_lo=xt_lo_late, prod=prod_late, w_diag=w_diag_late)
        late1 = dict(z_hi=z_hi1, z_lo=z_lo1, sel=sel1, w_hi=w_hi1, w_lo=w_lo1, b2=b2_col1, xt=xt1, xt_hi=xt_hi1,
                     xt_lo=xt_lo1, prod=prod_late, w_diag=w_diag_late)
        hid0 = (hf, h_hi, h_lo)
        hid1 = (hf1, h_hi1, h_lo1)

        def is_late(f):
            return isinstance(f, int) and f >= B

        def ffn_set(f):
            return (late1 if f % 2 else late0) if is_late(f) else ffn0

        def xt_slot(f, c):
            return c if is_late(f) else c % 2

        def ffn_input(f):
            if isinstance(f, int) and f > B:
                return ((xa1, s_xa1, 16), (x1p, s_xa2, 16), (xa, s_xa, 16 * (B + 2)))[f - B - 1]
            return xa, s_xa, 16 * (f + 1)

        def hid_set(f, c):
            return hid1 if is_late(f) and c % 2 else hid0

        banks = [ctx.enter_context(nc.psum_tensor(f"bank{i}", [P, 512], F32)) for i in range(8)]
        in_bank = banks[0:4]
        t_bank = banks[4:6]
        o_bank = banks[6:8]

        s_small = sem("s_small")
        s_xr = [sem(f"s_xr{i}") for i in range(2)]
        SW_PARTS = [1, 1, 4, 4]
        s_sw = [[sem(f"s_sw{t}_{i}") for i in range(parts)] for t, parts in enumerate(SW_PARTS)]
        s_xa = sem("s_xa")
        s_xa1 = sem("s_xa1")
        s_xa2 = sem("s_xa2")
        s_raw = [sem(f"s_raw{i}") for i in range(6)]
        s_x2 = sem("s_x2")
        s_out = [sem(f"s_out{t}") for t in range(NT)]
        s_pc = sem("s_pc")
        s_b3 = sem("s_b3")
        s_w3h = sem("s_w3h")
        s_whi = sem("s_whi")
        s_wlo = sem("s_wlo")
        s_wlp = sem("s_wlp")
        s_rv = sem("s_rv")
        s_rp = sem("s_rp")
        s_rn = sem("s_rn")
        s_rm = sem("s_rm")
        s_mix = sem("s_mix")
        s_lg = sem("s_lg")
        s_sh = sem("s_sh")
        s_exp = sem("s_exp")
        s_sel = [sem("s_sel1"), sem("s_sel2")]
        s_xn = sem("s_xn")
        s_xb = sem("s_xb")
        s_t1 = sem("s_t1")
        s_t1e = sem("s_t1e")
        s_xtl = sem("s_xtl")
        s_h = sem("s_h")
        s_gelu = sem("s_gelu")
        s_hh = sem("s_hh")
        s_hl = sem("s_hl")
        s_ob = sem("s_ob")
        s_obf = sem("s_obf")
        s_zh = sem("s_zh")
        s_zl = sem("s_zl")
        s_v1 = sem("s_v1")
        s_p1 = sem("s_p1")
        s_xn1 = sem("s_xn1")
        s_t2 = sem("s_t2")
        s_t2h = sem("s_t2h")
        s_t2a = sem("s_t2a")
        s_t2v = sem("s_t2v")
        s_in = sem("s_in")
        s_ina = sem("s_ina")
        s_u = sem("s_u")
        s_sq = sem("s_sq")
        s_ms = sem("s_ms")
        s_mse = sem("s_mse")
        s_rs = sem("s_rs")
        s_rsw = sem("s_rsw")
        s_rst = sem("s_rst")
        s_qn = sem("s_qn")
        s_qm = sem("s_qm")
        s_gv = sem("s_gv")
        s_w = sem("s_w")
        s_y = sem("s_y")
        s_yh = sem("s_yh")
        s_yl = sem("s_yl")
        s_ve = sem("s_ve")
        s_po = sem("s_po")

        FIRST = ["O0", "O1", "O2", "O3", "W0", "W1", "W2", "W3"]
        ROW = ["A0", "A1", "O0", "O1", "O2", "O3", "A2", "W0", "W1", "W2", "W3", "A3"]
        row_base = len(FIRST)
        last_base = row_base + (B - 1) * len(ROW)
        late_base = last_base + NT

        def bank_of(job, name=None):
            return {"A2": t_bank[0], "last A2": t_bank[0], "last A3": t_bank[1]}.get(name, o_bank[job % 2])

        def job_first(name):
            return FIRST.index(name)

        def job_row(b, name):
            return b * len(ROW) + (row_base + ROW.index(name))

        def job_last(name):
            return last_base + int(name[1])

        def job_late(f, name):
            n, r = int(name[1]), f - B
            if name[0] == "O":
                return late_base + (n if r == 0 else KC + 8 * (r - 1) + 2 * n + 1)
            return late_base + KC + (8 * r + 2 * n if r < B - 1 else 8 * (B - 1) + n)

        EVENTS = [(0, t, 0, B) for t in range(NT)]
        EVENTS += [(1, 0, 0, B - 1), (1, 1, 0, B - 1), (1, 0, B - 1, B), (1, 1, B - 1, B),
                   (1, 2, 0, B - 1), (1, 2, B - 1, B), (1, 3, 0, B - 1), (1, 3, B - 1, B)]

        def event(phase, t, whole):
            return 1 + max(n for n, (p, u, lo, hi) in enumerate(EVENTS) if (p, u) == (phase, t)
                           and (whole or lo == 0))

        def mm3(pe, res, a_hi, a_lo, b_hi, b_lo, start, stop):
            pe.matmul(res, a_hi, b_hi, start=start, stop=False)
            pe.matmul(res, a_hi, b_lo, start=False, stop=False)
            return pe.matmul(res, a_lo, b_hi, start=False, stop=stop)

        block = ctx.enter_context(nc.Block())

        @block.sync
        def _(sp):
            def row_of(src, f):
                return src[f].rearrange("(t p) d -> p t d", p=P)

            def chunk_load(src, t, rows):
                dst = xa if t % 2 == 0 else x1p
                sp.dma_start(dst[:, 0:rows], src[0:rows, t * P:(t + 1) * P, :].rearrange("b p d -> p b d")
                             ).then_inc(s_xr[t % 2], 16)

            def weight_load(t):
                n = E * D // SW_PARTS[t]
                src = switch_w[:, t].rearrange("p d e c -> p (d e c)")
                dst = route_w[:, t].rearrange("p d e c -> p (d e c)")
                for i in range(SW_PARTS[t]):
                    sp.dma_start(dst[:, i * n:(i + 1) * n], src[:, i * n:(i + 1) * n]).then_inc(s_sw[t][i], 16)

            def table_loads():
                for n, (w, bias) in enumerate(((w1, b1), (w2, b2))):
                    sp.dma_start(tab[n][:, 0:HD, :], w.partition_broadcast(HPC)).then_inc(s_small, 16)
                    sp.dma_start(tab[n][:, HD, :], bias.partition_broadcast(HPC)).then_inc(s_small, 16)
                sp.dma_start(b3_half[:], b3.partition_broadcast(P)).then_inc(s_small, 16)
                sp.dma_start(sw_bias[:], switch_b.partition_broadcast(P)).then_inc(s_small, 16)

            for t in range(2):
                chunk_load(x, t, B)
                weight_load(t)
            for t in range(2, NT):
                sp.wait_ge(s_rn, event(0, t - 2, True))
                chunk_load(x, t, B)
            for t in range(2, NT):
                weight_load(t)
            table_loads()
            sp.wait_ge(s_rn, event(0, 2, True))
            sp.dma_start(xa[:], row_of(x, 0)).then_inc(s_xa, 16)
            sp.dma_start(raw[:, 0, 0:KC * D].rearrange("p (k n) -> p k n", k=KC), w3).then_inc(s_raw[0], 16)
            sp.dma_start(raw[:, 1, 0:KC * D].rearrange("p (k n) -> p k n", k=KC), w_out).then_inc(s_raw[1], 16)
            sp.wait_ge(s_rn, event(0, 3, True))
            sp.dma_start(raw[:, 2, :], w_in[0]).then_inc(s_raw[2], 16)
            for g, split, n in ((1, s_wlp, 1), (2, s_wlp, 2), (3, s_wlo, 1)):
                sp.wait_ge(split, n)
                sp.dma_start(raw[:, (g + 2) % 3, :], w_in[g]).then_inc(s_raw[2 + g], 16)

            def store_x2(b, t, src, job):
                sp.wait_ge(s_obf, job + 1)
                sp.dma_start(x2_dram[b, t * P:(t + 1) * P, :], src[:, t, :]).then_inc(s_x2, 16)

            with sp.Fori(0, B - 1) as b:
                sp.wait_ge(s_obf, b * len(ROW) + row_base)
                sp.dma_start(xa[:], row_of(x, b + 1)).then_inc(s_xa, 16)
                for t in range(NT):
                    store_x2(b, t, x1p, job_row(b, f"A{t}"))

            sp.wait_ge(s_x2, 16 * NT * (B - 1))
            sp.wait_ge(s_obf, last_base)
            chunk_load(x2_dram, 0, B - 1)
            chunk_load(x2_dram, 1, B - 1)
            sp.wait_ge(s_rn, event(1, 0, False))
            chunk_load(x2_dram, 2, B - 1)
            sp.wait_ge(s_rn, event(1, 1, False))
            chunk_load(x2_dram, 3, B - 1)
            sp.wait_ge(s_in, IN_JOBS * B)
            for t in range(NT - 1):
                weight_load(t)
            sp.wait_ge(s_y, KC * B)
            weight_load(NT - 1)
            for t in range(NT):
                store_x2(B - 1, t, x1, job_last(f"A{t}"))
            sp.wait_ge(s_rn, event(1, 2, False))
            sp.dma_start(xa[:], row_of(x2_dram, 0)).then_inc(s_xa, 16)
            sp.wait_ge(s_rm, 2 * NT)
            sp.dma_start(xa1[:], row_of(x2_dram, 1)).then_inc(s_xa1, 16)
            sp.dma_start(x1p[:], row_of(x2_dram, 2)).then_inc(s_xa2, 16)
            for f in range(B, 2 * B):
                for t in range(NT):
                    sp.wait_ge(s_obf, job_late(f, f"W{t}") + 1)
                    sp.dma_start(out[f - B, t * P:(t + 1) * P, :], x1[:, t, :]).then_inc(s_out[t], 16)
                if f == B:
                    sp.wait_ge(s_x2, 16 * NT * B)
                    sp.dma_start(xa[:], row_of(x2_dram, B - 1)).then_inc(s_xa, 16)
            for t in range(NT):
                sp.wait_ge(s_out[t], 16 * B)

        @block.tensor
        def _(pe):
            def route(phase):
                if phase == 1:
                    pe.wait_ge(s_obf, last_base + 1)
                for t in range(NT):
                    pe.wait_ge(s_rn, event(phase, t, True))
                    xn = xnw if t % 2 == 0 else xnr
                    for d in range(D // HD):
                        if d % (D // HD // SW_PARTS[t]) == 0:
                            pe.wait_ge(s_sw[t][d // (D // HD // SW_PARTS[t])], 16 * (phase + 1))
                        mm = pe.matmul(o_bank[0][:, 0:E * HD], xn[:, d * P:(d + 1) * P],
                                       route_w[:, t, d],
                                       start=(t == 0 and d == 0), stop=(t == NT - 1 and d == D // HD - 1))
                    mm.then_inc(s_rm, 1)

            def logits(phase):
                if phase == 1:
                    pe.wait_ge(s_obf, last_base + 2)
                pe.wait_ge(s_mix, phase + 1)
                pe.matmul(o_bank[1][:, 0:B * E], ones[:], lmix[:].rearrange("p b e -> p (b e)"),
                          start=True, stop=True).then_inc(s_lg, 1)

            def t1(f, c, after_row, after_ffn):
                if c == 0:
                    pe.wait_ge(s_xn, NT * (f + 1))
                if c >= 2:
                    pe.wait_ge(s_t1e, KC * f + c - 1)
                elif after_row is not None:
                    pe.wait_ge(s_mse if c == 0 else s_qn, KC * (after_row + 1))
                elif after_ffn:
                    pe.wait_ge(s_t1e, KC * f - 1 + c)
                for t in range(NT):
                    tp = pe.transpose(t_bank[c % 2][:, t * P:(t + 1) * P],
                                      xnw[:, t * D + c * P:t * D + (c + 1) * P], ident[:])
                tp.then_inc(s_t1, 1)

            def hidden(f, c, after_row, after_ffn):
                use = ffn_set(f)
                if c == 0:
                    pe.wait_ge(s_sel[0], f + 1)
                pe.wait_ge(s_t1e, KC * f + c + 1)
                pe.wait_ge(s_xtl, KC * f + c + 1)
                for k in range(TOPK):
                    j = TOPK * c + k
                    if j >= 4:
                        pe.wait_ge(s_gelu, H_JOBS * f + j - 3)
                    elif after_row is not None:
                        pe.wait_ge(s_ina, IN_JOBS * after_row + 17 + j)
                        if j == 2:
                            pe.wait_ge(s_u, KC * (after_row + 1))
                    elif after_ffn:
                        pe.wait_ge(s_gelu, H_JOBS * f - 3 + j)
                    mm3(pe, in_bank[j % 4][:], use["w_hi"][0][:, k, :], use["w_lo"][0][:, k, :],
                        use["xt_hi"][:, xt_slot(f, c), :], use["xt_lo"][:, xt_slot(f, c), :], True, True).then_inc(s_h, 1)

            def bank_free(job):
                pe.wait_ge(s_obf, job - 1)

            def experts_out(f, c, job, bank, first=False):
                use = ffn_set(f)
                if c == 0:
                    pe.wait_ge(s_sel[1], f + 1)
                if not first:
                    bank_free(job)
                _, hi, lo = hid_set(f, c)
                for k in range(TOPK):
                    pe.wait_ge(s_hl, H_JOBS * f + TOPK * c + k + 1)
                    mm = mm3(pe, bank[:], use["w_hi"][1][:, k, :], use["w_lo"][1][:, k, :], hi[:, k, :],
                             lo[:, k, :], k == 0, k == TOPK - 1)
                mm.then_inc(s_ob, 1)

            def project(t, bank, a_hi, a_lo, w_hi, w_lo, chunks=range(KC), chunk_wait=lambda k: None):
                tok = slice(t * P, (t + 1) * P)
                for k in chunks:
                    chunk_wait(k)
                    mm = mm3(pe, bank[:], a_hi[:, k, tok], a_lo[:, k, tok], w_hi[:, k, :], w_lo[:, k, :],
                             k == 0, k == KC - 1)
                if chunks[-1] == KC - 1:
                    mm.then_inc(s_ob, 1)

            def w3_tile(f, t, job, bank):
                use = ffn_set(f)

                def z_ready(k):
                    if t == 0:
                        pe.wait_ge(s_zh, KC * f + k + 1)
                        pe.wait_ge(s_zl, KC * f + k + 1)

                bank_free(job)
                project(t, bank, use["z_hi"], use["z_lo"], w3_hi, w3_lo, chunk_wait=z_ready)

            def out_tile(b, t, bank, chunks=range(KC)):
                if t == 0:
                    pe.wait_ge(s_yh, KC * b + chunks[-1] + 1)
                    pe.wait_ge(s_yl, KC * b + chunks[-1] + 1)
                project(t, bank, y_hi, y_lo, wo_hi, wo_lo, chunks)

            def t2(b, t):
                if t == 0:
                    pe.wait_ge(s_gelu, H_JOBS * (b + 1))
                pe.wait_ge(s_xn1, NT * b + t + 1)
                for c in range(KC):
                    tp = pe.transpose(in_bank[t][:, c * P:(c + 1) * P],
                                      xnw[:, t * D + c * P:t * D + (c + 1) * P], ident[:])
                tp.then_inc(s_t2, 1)

            def in_part(b, first):
                for c in range(KC):
                    if first:
                        pe.wait_ge(s_whi, 3 + c)
                        if c < 3:
                            pe.wait_ge(s_wlo, (1, 3, 2)[c])
                        else:
                            pe.wait_ge(s_wlp, 3)
                    for r in range(ROLES):
                        j = ROLES * c + r
                        bank = in_bank[j % 4]
                        if j >= 4:
                            pe.wait_ge(s_ina, IN_JOBS * b + j - 3)
                            if (j - 4) % ROLES == JOB_V:
                                pe.wait_ge(s_u, KC * b + (j - 4) // ROLES + 1)
                        if j == 0:
                            pe.wait_ge(s_t2h, NT * (b + 1))
                            for k in range(KC):
                                pe.matmul(bank[:], win_hi[:, c, r, k, :], xh[:, k, :], start=(k == 0), stop=False)
                            pe.wait_ge(s_t2v, NT * (b + 1))
                            for k in range(KC):
                                pe.matmul(bank[:], win_hi[:, c, r, k, :], xl[:, k, :], start=False, stop=False)
                            pe.wait_ge(s_t2a, NT * (b + 1))
                        else:
                            for k in range(KC):
                                pe.matmul(bank[:], win_hi[:, c, r, k, :], xh[:, k, :], start=(k == 0), stop=False)
                                pe.matmul(bank[:], win_hi[:, c, r, k, :], xl[:, k, :], start=False, stop=False)
                        for k in range(KC):
                            mm = pe.matmul(bank[:], win_lo[:, c, r, k, :], xbf[:, k, :], start=False,
                                           stop=(k == KC - 1))
                        mm.then_inc(s_in, 1)
                        if r == JOB_A:
                            pe.wait_ge(s_sq, KC * b + c + 1)
                            if c >= 1:
                                pe.wait_ge(s_mse, KC * b + c)
                            for t in range(NT):
                                mm = pe.matmul(t_bank[0][:, t * HPC:(t + 1) * HPC], q_sq[:, t * P:(t + 1) * P],
                                               head_of[:], start=True, stop=True)
                            mm.then_inc(s_ms, 1)
                        if r == (JOB_V if c == KC - 1 else JOB_G):
                            pe.wait_ge(s_rsw, KC * b + c + 1)
                            if c >= 1:
                                pe.wait_ge(s_qn, KC * b + c)
                            for t in range(NT):
                                mm = pe.transpose(t_bank[1][:, t * P:(t + 1) * P],
                                                  rs_wide[:, t].rearrange("p j c -> p (j c)"), ident[:])
                            mm.then_inc(s_rst, 1)

            def row_end(b):
                f = b + 1

                def do(name, chunks=range(KC)):
                    job, n = job_row(b, name), int(name[1])
                    bank = bank_of(row_base + ROW.index(name), name)
                    if name[0] == "O":
                        experts_out(f, n, job, bank)
                    elif name[0] == "W":
                        w3_tile(f, n, job, bank)
                    else:
                        if chunks[0] == 0 and bank in o_bank:
                            bank_free(job)
                        out_tile(b, n, bank, chunks)

                for c in range(KC):
                    t1(f, c, b, False)
                    if c < 2:
                        do(f"A{c}", range(KC - 1))
                hidden(f, 0, b, False)
                hidden(f, 1, b, False)
                for name in ("A0", "A1"):
                    do(name, range(KC - 1, KC))
                do("O0")
                hidden(f, 2, b, False)
                do("O1")
                hidden(f, 3, b, False)
                do("O2")
                do("A2", range(2))
                do("O3")
                do("A2", range(2, KC))
                for t in range(NT - 1):
                    do(f"W{t}")
                t2(f, 0)
                do("W3")
                t2(f, 1)
                do("A3", range(2))
                t2(f, 2)
                do("A3", range(2, KC))
                t2(f, 3)

            pe.wait_ge(s_pc, 1)
            route(0)
            for c in range(KC):
                t1(0, c, None, False)
                if c == 1:
                    logits(0)
            hidden(0, 0, None, False)
            hidden(0, 1, None, False)
            for c in range(KC):
                job = job_first(f"O{c}")
                experts_out(0, c, job, bank_of(job), c < 2)
                if c < 2:
                    hidden(0, c + 2, None, False)
            pe.wait_ge(s_whi, 1)
            pe.wait_ge(s_wlp, 1)
            for t in range(NT):
                if t == 3:
                    t2(0, 0)
                job = job_first(f"W{t}")
                w3_tile(0, t, job, bank_of(job))
            for t in range(1, NT):
                t2(0, t)
            in_part(0, True)
            row_end(0)
            with pe.Fori(1, B - 1) as b:
                in_part(b, False)
                row_end(b)
            in_part(B - 1, False)
            for chunks in (range(KC - 1), range(KC - 1, KC)):
                for t in range(NT):
                    if chunks[0] == 0:
                        if t < 2:
                            bank_free(job_last(f"A{t}"))
                        else:
                            pe.wait_ge(s_mse if t == 2 else s_qn, KC * B)
                    out_tile(B - 1, t, bank_of(job_last(f"A{t}"), f"last A{t}"), chunks)
            route(1)
            pe.wait_ge(s_obf, late_base)
            for c in range(KC):
                t1(B, c, B - 1, False)
                if c == 1:
                    logits(1)
            hidden(B, 0, B - 1, False)
            hidden(B, 1, B - 1, False)
            for f in range(B, 2 * B):
                for c in range(KC):
                    if f > B:
                        job = job_late(f - 1, f"W{c}")
                        w3_tile(f - 1, c, job, bank_of(job))
                    job = job_late(f, f"O{c}")
                    experts_out(f, c, job, bank_of(job))
                    if c < 2:
                        hidden(f, c + 2, B - 1, f > B)
                    if f + 1 < 2 * B:
                        if c in (1, 2):
                            t1(f + 1, 2 * c - 2, None, True)
                            t1(f + 1, 2 * c - 1, None, True)
                        if c == 3:
                            hidden(f + 1, 0, None, True)
                            hidden(f + 1, 1, None, True)
            for t in range(NT):
                job = job_late(2 * B - 1, f"W{t}")
                w3_tile(2 * B - 1, t, job, bank_of(job))

        @block.scalar
        def _(act):
            def load_table(func):
                act.activation(table_out[:], two[:], func)

            def route_exp(phase):
                act.wait_ge(s_sh, phase + 1)
                act.activation(probs[:], lg[:], ACT.Exp).then_inc(s_exp, 1)

            def t1_out(f, c):
                use = ffn_set(f)
                act.wait_ge(s_t1, KC * f + c + 1)
                if is_late(f) and f > B + 1:
                    if c == 0:
                        act.wait_ge(s_zl, KC * (f - 1))
                        act.wait_ge(s_h, H_JOBS * (f - 1))
                elif c == 0 and not (isinstance(f, int) and f in (0, B + 1)):
                    act.wait_ge(s_zl, KC * f)
                act.activation(use["xt"][:, c, :], t_bank[c % 2][:], ACT.Copy)
                act.activation(use["xt_hi"][:, xt_slot(f, c), :], t_bank[c % 2][:], ACT.Copy).then_inc(s_t1e, 1)

            def gelu(f, c):
                for k in range(TOPK):
                    act.wait_ge(s_h, H_JOBS * f + TOPK * c + k + 1)
                    if is_late(f) or not (isinstance(f, int) and f == 0 and c == 0):
                        bufs = 2 if is_late(f) else 1
                        act.wait_ge(s_hl, H_JOBS * f + TOPK * (c - bufs) + k + 1)
                    act.activation(hid_set(f, c)[0][:, k, :], in_bank[(TOPK * c + k) % 4][:], ACT.Gelu,
                                   bias=ffn_set(f)["sel"][0][:, k, HD:FB]).then_inc(s_gelu, 1)

            def hidden_hi(f, c, read_job):
                src, hi, _ = hid_set(f, c)
                if read_job is not None:
                    act.wait_ge(s_ob, read_job + 1)
                for k in range(TOPK):
                    act.wait_ge(s_gelu, H_JOBS * f + TOPK * c + k + 1)
                    act.activation(hi[:, k, :], src[:, k, :], ACT.Copy).then_inc(s_hh, 1)

            def z_out(f, c, job):
                act.wait_ge(s_obf, job + 1)
                if is_late(f) and f >= B + 2 and c == 0:
                    act.wait_ge(s_ob, job_late(f - 2, "W3") + 1)
                use = ffn_set(f)
                act.activation(use["z_hi"][:, c, :], use["xt"][:, c, :], ACT.Copy).then_inc(s_zh, 1)

            def ffn(f, job, begun=lambda: None, between=lambda: None):
                t1_out(f, 0)
                t1_out(f, 1)
                begun()
                gelu(f, 0)
                t1_out(f, 2)
                gelu(f, 1)
                t1_out(f, 3)
                between()
                gelu(f, 2)
                z_out(f, 0, job("O0"))
                gelu(f, 3)
                for c in range(1, KC):
                    z_out(f, c, job(f"O{c}"))

            def t2_out(b):
                for t in range(NT):
                    act.wait_ge(s_t2, NT * b + t + 1)
                    src = in_bank[t][:].rearrange("p (c s) -> p c s", c=KC)
                    cols = slice(t * P, (t + 1) * P)
                    act.activation(xh[:, :, cols], src, ACT.Copy).then_inc(s_t2h, 1)
                    act.activation(xbf[:, :, cols], src, ACT.Copy).then_inc(s_t2a, 1)

            def y_out(b, c):
                act.wait_ge(s_y, KC * b + c + 1)
                act.activation(y_hi[:, c, :], yt[:], ACT.Copy).then_inc(s_yh, 1)

            def group(b, c):
                def bank(r):
                    act.wait_ge(s_in, IN_JOBS * b + ROLES * c + r + 1)
                    return in_bank[(ROLES * c + r) % 4][:]

                src = bank(JOB_Q)
                if c >= 1:
                    act.wait_ge(s_ms, KC * b + c)
                act.activation(q_sq[:], src, ACT.Square).then_inc(s_sq, 1)
                if c >= 1:
                    act.wait_ge(s_qm, KC * b + c)
                act.activation(qt[:], src, ACT.Copy).then_inc(s_ina, 1)
                src = bank(JOB_A)
                act.activation(decay[:], src, ACT.Sigmoid, bias=two[:]).then_inc(s_ina, 1)
                act.wait_ge(s_ms, KC * b + c + 1)
                if c >= 1:
                    act.wait_ge(s_rs, KC * b + c)
                act.activation(ms[:], t_bank[0][:, 0:NT * HPC], ACT.Identity, scale=1.0 / HD,
                               bias=rms_eps[:]).then_inc(s_mse, 1)
                src = bank(JOB_K)
                act.activation(kt[:], src, ACT.Tanh).then_inc(s_ina, 1)
                src = bank(JOB_V)
                if c >= 1:
                    act.wait_ge(s_y, KC * b + c)
                    y_out(b, c - 1)
                act.activation(vt[:], src, ACT.Copy).then_inc(s_ina, 1)
                src = bank(JOB_G)
                act.activation(gt[:], src, ACT.Sigmoid).then_inc(s_ina, 1)

            def attention(b):
                for c in range(KC):
                    group(b, c)

            def split_hi(i, dst, src):
                act.wait_ge(s_raw[i], 16)
                act.activation(dst, src, ACT.Copy).then_inc(s_whi, 1)

            def split_in(g):
                split_hi(2 + g, win_hi[:, g].rearrange("p r k n -> p (r k n)"), raw[:, (g + 2) % 3, :])

            def begun():
                w3_raw = raw[:, 0, 0:KC * D]
                act.wait_ge(s_raw[0], 16)
                act.activation(w3_raw, w3_raw, ACT.Copy, scale=0.5).then_inc(s_w3h, 1)
                route_exp(0)
                act.wait_ge(s_w3h, 1)
                split_hi(0, w3_hi[:].rearrange("p k n -> p (k n)"), w3_raw)
                split_hi(1, wo_hi[:].rearrange("p k n -> p (k n)"), raw[:, 1, 0:KC * D])

            act.wait_ge(s_small, 16 * 6)
            act.activation(b3_half[:], b3_half[:], ACT.Copy, scale=0.5).then_inc(s_b3, 1)
            act.wait_ge(s_pc, 1)
            ffn(0, job_first, begun, lambda: split_in(0))
            for g in range(1, KC):
                split_in(g)
            t2_out(0)
            load_table(ACT.Sigmoid)
            act.wait_ge(s_wlo, 2)
            act.wait_ge(s_wlp, 3)
            with act.Fori(0, B - 1) as b:
                attention(b)

                def begun():
                    y_out(b, KC - 1)
                    load_table(ACT.Gelu)

                ffn(b + 1, lambda name: job_row(b, name), begun)
                t2_out(b + 1)
                load_table(ACT.Sigmoid)
            attention(B - 1)
            y_out(B - 1, KC - 1)
            for c in range(KC):
                t1_out(B, c)
            route_exp(1)
            for c in range(2):
                gelu(B, c)
                hidden_hi(B, c, None)
            for f in range(B, 2 * B):
                for c in range(KC):
                    z_out(f, c, job_late(f, f"O{c}"))
                    if f + 1 < 2 * B:
                        if c in (1, 2):
                            t1_out(f + 1, 2 * c - 2)
                            t1_out(f + 1, 2 * c - 1)
                        if c == 3:
                            for n in range(2):
                                gelu(f + 1, n)
                                hidden_hi(f + 1, n, job_late(f, f"O{n + 2}"))
                    if c < 2:
                        gelu(f, c + 2)
                        hidden_hi(f, c + 2, job_late(f, f"O{c}"))

        @block.gpsimd
        def _(pool):
            own = Steps(pool, s_po)
            for ap, value in ((ident, 0.0), (diag, 0.0), (head_of, 1.0), (neg_half, -0.5), (two, 2.0), (ones, 1.0),
                              (rms_eps, RMS_EPS)):
                own.mark(pool.memset(ap[:], value))
            for e in range(E):
                own.mark(pool.memset(rank[:, e:e + 1], float(E - e)))
            own.wait(own.n)
            own.mark(pool.affine_select(out=ident[:], in_=ident[:], compare_op=ALU.not_equal, fill=1.0, base=0,
                                        pattern=[[-1, P]], channel_multiplier=1))
            for j in range(HPC):
                own.do(pool.affine_select(out=diag[:], in_=diag[:], compare_op=ALU.not_equal, fill=1.0,
                                          base=-HD * j, pattern=[[-1, HD]], channel_multiplier=1))
            own.do(pool.affine_select(out=head_of[:], in_=head_of[:], compare_op=ALU.is_ge, fill=0.0, base=0,
                                      pattern=[[-HD, HPC]], channel_multiplier=1))
            pool.affine_select(out=head_of[:], in_=head_of[:], compare_op=ALU.is_ge, fill=0.0, base=HD - 1,
                               pattern=[[HD, HPC]], channel_multiplier=-1).then_inc(s_pc, 1)

            def route_rstd(n):
                _, t, lo, hi = EVENTS[n]
                pool.wait_ge(s_rv, n + 1)
                pool.tensor_tensor(rstd[:, lo:hi, t], mv[:, lo:hi, t, 1], neg_half[:, 0:hi - lo],
                                   ALU.pow).then_inc(s_rp, 1)

            def xt_split(f, c):
                pool.wait_ge(s_t1e, KC * f + c + 1)
                if c >= 2 and not is_late(f):
                    pool.wait_ge(s_h, H_JOBS * f + TOPK * (c - 1))
                use, slot = ffn_set(f), xt_slot(f, c)
                pool.tensor_tensor(use["xt_lo"][:, slot, :], use["xt"][:, c, :], use["xt_hi"][:, slot, :],
                                   ALU.subtract).then_inc(s_xtl, 1)

            def z_split(f, c):
                use = ffn_set(f)
                pool.wait_ge(s_zh, KC * f + c + 1)
                pool.tensor_tensor(use["z_lo"][:, c, :], use["xt"][:, c, :], use["z_hi"][:, c, :],
                                   ALU.subtract).then_inc(s_zl, 1)

            def residual_bias(f, t):
                ap = ffn_input(f)[0][:, t, :]
                pool.wait_ge(s_xn, NT * f + t + 1)
                pool.tensor_tensor(ap, ap, b3_half[:], ALU.add).then_inc(s_xb, 1)

            def ln_rstd(b):
                for t in range(NT):
                    pool.wait_ge(s_v1, NT * b + t + 1)
                    pool.tensor_tensor(rstd1[:, t:t + 1], mv1[:, t, 1:2], neg_half[:, 0:1],
                                       ALU.pow).then_inc(s_p1, 1)

            def group(b, c):
                pool.wait_ge(s_mse, KC * b + c + 1)
                if c >= 1:
                    pool.wait_ge(s_rsw, KC * b + c)
                pool.tensor_tensor(rs[:], ms[:], neg_half[:], ALU.pow).then_inc(s_rs, 1)
                pool.wait_ge(s_rs, KC * b + c + 1)
                if c >= 1:
                    pool.wait_ge(s_rst, KC * b + c)
                pool.tensor_tensor(rs_wide[:].rearrange("p t j c -> p (t j) c"),
                                   rs[:].unsqueeze(2).to_broadcast([P, NT * HPC, HD]),
                                   ones[:, 0:1].unsqueeze(2).to_broadcast([P, NT * HPC, HD]),
                                   ALU.mult).then_inc(s_rsw, 1)
                pool.wait_ge(s_ina, IN_JOBS * b + ROLES * c + JOB_G + 1)
                pool.tensor_tensor(gv[:], gt[:], vt[:], ALU.mult).then_inc(s_gv, 1)
                pool.wait_ge(s_gv, KC * b + c + 1)
                pool.tensor_tensor(vt[:], vt[:], gv[:], ALU.subtract).then_inc(s_w, 1)

            def split_lo(i, dst, src, hi):
                pool.wait_ge(s_whi, i + 1)
                pool.tensor_tensor(dst, src, hi, ALU.subtract).then_inc(s_wlp, 1)

            for n in range(NT):
                route_rstd(n)
            pool.wait_ge(s_b3, 1)
            for t in range(NT):
                residual_bias(0, t)
            xt_split(0, 0)
            xt_split(0, 1)
            split_lo(0, w3_lo[:].rearrange("p k n -> p (k n)"), raw[:, 0, 0:KC * D],
                     w3_hi[:].rearrange("p k n -> p (k n)"))
            xt_split(0, 2)
            xt_split(0, 3)
            split_lo(1, wo_lo[:].rearrange("p k n -> p (k n)"), raw[:, 1, 0:KC * D],
                     wo_hi[:].rearrange("p k n -> p (k n)"))
            for c in range(KC):
                z_split(0, c)
            ln_rstd(0)
            split_lo(5, win_lo[:, 3].rearrange("p r k n -> p (r k n)"), raw[:, 2, :],
                     win_hi[:, 3].rearrange("p r k n -> p (r k n)"))
            with pool.Fori(0, B - 1) as b:
                for c in range(KC):
                    group(b, c)
                    if c == 2:
                        residual_bias(b + 1, 0)
                        residual_bias(b + 1, 1)
                xt_split(b + 1, 0)
                xt_split(b + 1, 1)
                residual_bias(b + 1, 2)
                xt_split(b + 1, 2)
                xt_split(b + 1, 3)
                residual_bias(b + 1, 3)
                for c in range(KC):
                    z_split(b + 1, c)
                ln_rstd(b + 1)
            for c in range(KC):
                group(B - 1, c)
                if c in (1, 2):
                    route_rstd(NT + c - 1)
            for n in range(NT + 2, len(EVENTS)):
                route_rstd(n)
            for c in range(KC):
                xt_split(B, c)
            for f in range(B, 2 * B):
                for c in range(KC):
                    z_split(f, c)
                    residual_bias(f, c)
                    if f + 1 < 2 * B and c in (1, 2):
                        xt_split(f + 1, 2 * c - 2)
                        xt_split(f + 1, 2 * c - 1)

        @block.vector
        def _(ve):
            own = Steps(ve, s_ve)

            def route_event(n):
                phase, t, lo, hi = EVENTS[n]
                slot = xa if t % 2 == 0 else x1p
                xn = xnw if t % 2 == 0 else xnr
                if lo == 0:
                    ve.wait_ge(s_xr[t % 2], 16 * (2 * phase + t // 2 + 1))

                def src(b):
                    return x1[:, t, :] if lo > 0 else slot[:, b, :]

                for b in range(lo, hi):
                    m = own.mark(ve.bn_stats(stats[:, b, :], src(b)))
                own.wait(m)
                for b in range(lo, hi):
                    m = own.mark(ve.bn_aggr(mv[:, b, t, :], stats[:, b, :]))
                own.wait(m)
                ve.tensor_scalar(mv[:, lo:hi, t, 1], mv[:, lo:hi, t, 1], LN_EPS, None, ALU.add).then_inc(s_rv, 1)
                ve.wait_ge(s_rp, n + 1)
                if t >= 2:
                    ve.wait_ge(s_rm, NT * phase + t - 1)
                for b in range(lo, hi):
                    dst = xn[:].rearrange("p (d b c) -> p d b c", b=B, c=HD)[:, :, b, :]
                    ins = ve.tensor_scalar(dst, src(b).rearrange("p (d c) -> p d c", c=HD),
                                           mv[:, b, t, 0:1], rstd[:, b, t:t + 1], ALU.subtract, ALU.mult)
                ins.then_inc(s_rn, 1)

            def choose(phase):
                def over_e(ap):
                    return ap.unsqueeze(2).to_broadcast([P, B, E])

                ve.wait_ge(s_rm, NT * (phase + 1))
                acc = o_bank[0][:, 0:E * HD].rearrange("p (e c) -> p e c", e=E)
                scratch = prod[:].rearrange("p k f e -> p (k f e)")[:, 0:E * HD].rearrange("p (e c) -> p e c", e=E)
                own.do(ve.tensor_tensor(scratch, acc, diag[:].unsqueeze(1).to_broadcast([P, E, HD]), ALU.mult))
                own.do(ve.tensor_reduce(part[:], scratch, AX.X, ALU.add))
                ve.tensor_tensor(lmix[:], part[:].unsqueeze(1).to_broadcast([P, B, E]), over_e(head_of[:]),
                                 ALU.mult).then_inc(s_mix, 1)
                ve.wait_ge(s_lg, phase + 1)
                own.do(ve.tensor_tensor(lg[:], o_bank[1][:, 0:B * E].rearrange("p (b e) -> p b e", b=B),
                                        sw_bias[:].unsqueeze(1).to_broadcast([P, B, E]), ALU.add))
                rank_b = rank[:].unsqueeze(1).to_broadcast([P, B, E])
                for k, of in enumerate((lg, lg2)):
                    own.do(ve.tensor_reduce(red[:], of[:], AX.X, ALU.max))
                    ins = ve.tensor_tensor(of[:], of[:], over_e(red[:]), ALU.subtract)
                    if k == 0:
                        ins.then_inc(s_sh, 1)
                        ve.wait_ge(s_sh, phase + 1)
                    else:
                        own.do(ins)
                    own.do(ve.scalar_tensor_tensor(out=eq[:], in0=of[:], scalar=0.0, in1=rank_b,
                                                   op0=ALU.is_equal, op1=ALU.mult))
                    own.do(ve.tensor_reduce(red[:], eq[:], AX.X, ALU.max))
                    own.do(ve.tensor_tensor(pick[:, :, k, :], eq[:], over_e(red[:]), ALU.is_equal))
                    if k == 0:
                        own.do(ve.scalar_tensor_tensor(out=lg2[:], in0=pick[:, :, 0, :], scalar=TAKEN, in1=lg[:],
                                                       op0=ALU.mult, op1=ALU.add))

            def gate(phase):
                ve.wait_ge(s_exp, phase + 1)
                own.do(ve.tensor_reduce(red[:], probs[:], AX.X, ALU.add))
                own.do(ve.reciprocal(red[:], red[:]))
                own.do(ve.tensor_tensor(probs[:], probs[:], red[:].unsqueeze(2).to_broadcast([P, B, E]), ALU.mult))
                for k in range(TOPK):
                    m = own.mark(ve.tensor_tensor(pick_g[:, :, k, :], pick[:, :, k, :], probs[:], ALU.mult))
                own.wait(m)

            def select(row, f, n):
                use = ffn_set(f)
                prod, w_diag, choice = use["prod"], use["w_diag"], (pick, pick_g)[n]
                sel, hi, lo = use["sel"][n], use["w_hi"][n], use["w_lo"][n]
                for k in range(TOPK):
                    m = own.mark(ve.tensor_tensor(
                        prod[:, k], tab[n][:],
                        choice[:, bass.ds(row, 1), k, :].to_broadcast([P, FB, E]), ALU.mult))
                own.wait(m)
                own.do(ve.tensor_reduce(sel[:], prod[:], AX.X, ALU.add))
                for k in range(TOPK):
                    m = own.mark(ve.tensor_tensor(
                        w_diag[:, k], sel[:, k, 0:HD].unsqueeze(1).to_broadcast([P, HPC, HD]),
                        head_of[:].unsqueeze(2).to_broadcast([P, HPC, HD]), ALU.mult))
                if n == 1:
                    m = own.mark(ve.tensor_tensor(use["b2"][:], sel[:, 0, HD:FB], sel[:, 1, HD:FB], ALU.add))
                own.wait(m)
                own.do(ve.tensor_copy(hi[:].rearrange("p k (j c) -> p k j c", j=HPC), w_diag[:]))
                ve.tensor_tensor(lo[:].rearrange("p k (j c) -> p k j c", j=HPC), w_diag[:],
                                 hi[:].rearrange("p k (j c) -> p k j c", j=HPC),
                                 ALU.subtract).then_inc(s_sel[n], 1)
                ve.wait_ge(s_sel[n], f + 1)

            def normalise(f, row):
                src, *loaded = ffn_input(f)
                ve.wait_ge(*loaded)
                for t in range(NT):
                    ve.tensor_scalar(xnw[:, t * D:(t + 1) * D], src[:, t, :], mv[:, bass.ds(row, 1), t, 0],
                                     rstd[:, bass.ds(row, 1), t], ALU.subtract, ALU.mult).then_inc(s_xn, 1)

            def split_hidden(f, c, read_job):
                src, hi, lo = hid_set(f, c)
                for k in range(TOPK):
                    ve.wait_ge(s_gelu, H_JOBS * f + TOPK * c + k + 1)
                    if k == 0 and read_job is not None:
                        ve.wait_ge(s_ob, read_job + 1)
                    own.do(ve.tensor_copy(hi[:, k, :], src[:, k, :]))
                    ve.tensor_tensor(lo[:, k, :], src[:, k, :], hi[:, k, :], ALU.subtract).then_inc(s_hl, 1)

            def hidden_lo(f, c):
                src, hi, lo = hid_set(f, c)
                for k in range(TOPK):
                    ve.wait_ge(s_hh, H_JOBS * (f - B) + TOPK * c + k + 1)
                    ve.tensor_tensor(lo[:, k, :], src[:, k, :], hi[:, k, :], ALU.subtract).then_inc(s_hl, 1)

            def add_experts(f, c, job, bank):
                ve.wait_ge(s_ob, job + 1)
                use = ffn_set(f)
                ve.scalar_tensor_tensor(out=use["xt"][:, c, :], in0=bank[:], scalar=use["b2"][:],
                                        in1=use["xt"][:, c, :], op0=ALU.add, op1=ALU.add).then_inc(s_obf, 1)

            def w3_add(f, t, job, bank):
                ve.wait_ge(s_xb, NT * f + t + 1)
                ve.wait_ge(s_ob, job + 1)
                ve.tensor_tensor(x1[:, t, :], bank[:], ffn_input(f)[0][:, t, :],
                                 ALU.add).then_inc(s_obf, 1)

            def norm1(f, t):
                ve.wait_ge(s_p1, NT * f + t + 1)
                ve.tensor_scalar(xnw[:, t * D:(t + 1) * D], x1[:, t, :], mv1[:, t, 0:1], rstd1[:, t:t + 1],
                                 ALU.subtract, ALU.mult).then_inc(s_xn1, 1)

            def w3_norm(f, t, job, bank):
                w3_add(f, t, job, bank)
                ve.wait_ge(s_obf, job + 1)
                m = own.mark(ve.bn_stats(stats[:, t, :], x1[:, t, :]))
                own.wait(m)
                if t >= 1:
                    norm1(f, t - 1)
                else:
                    ve.tensor_copy(fence[:], neg_half[:, 0:1])
                own.do(ve.bn_aggr(mv1[:, t, :], stats[:, t, :]))
                ve.tensor_scalar(mv1[:, t, 1:2], mv1[:, t, 1:2], LN_EPS, None, ALU.add).then_inc(s_v1, 1)
                if t == NT - 1:
                    t2_lo(f, 0)
                    norm1(f, t)
                    for u in range(1, NT):
                        t2_lo(f, u)

            def out_add(t, job, bank, src, dst):
                ve.wait_ge(s_ob, job + 1)
                ve.tensor_tensor(dst[:, t, :], src[:, t, :], bank[:], ALU.add).then_inc(s_obf, 1)

            def t2_lo(b, t):
                ve.wait_ge(s_t2a, NT * b + t + 1)
                cols = slice(t * P, (t + 1) * P)
                ve.tensor_tensor(xl[:, :, cols], in_bank[t][:].rearrange("p (c s) -> p c s", c=KC),
                                 xh[:, :, cols], ALU.subtract).then_inc(s_t2v, 1)

            def group(b, c):
                job = IN_JOBS * b + ROLES * c
                ve.wait_ge(s_ina, job + JOB_A + 1)
                own.do(ve.tensor_scalar(decay[:], decay[:], A_MIN, A_MAX, ALU.max, ALU.min))
                first = decay[:].rearrange("p (n s) -> p n s", s=CHUNK)[:, :, 0:1]
                own.do(ve.tensor_scalar(starts[:].rearrange("p (n s) -> p n s", s=CHUNK)[:, :, 0:1], first,
                                        1.0 / GUARD, None, ALU.mult))
                pref_done = own.mark(ve.tensor_tensor_scan(pref[:], decay[:], starts[:], 0.0, ALU.mult, ALU.max))
                ve.wait_ge(s_ina, job + JOB_V + 1)
                ve.tensor_tensor(kt[:], kt[:], in_bank[(ROLES * c + JOB_V) % 4][:], ALU.mult).then_inc(s_u, 1)
                ve.wait_ge(s_u, KC * b + c + 1)
                own.wait(pref_done)
                in_done = own.mark(ve.scalar_tensor_tensor(out=pref[:], in0=pref[:], scalar=1.0, in1=kt[:],
                                                           op0=ALU.min, op1=ALU.mult))
                ve.wait_ge(s_rst, KC * b + c + 1)
                ve.tensor_tensor(qt[:], qt[:], t_bank[1][:], ALU.mult).then_inc(s_qn, 1)
                own.wait(in_done)
                own.do(ve.tensor_tensor_scan(kt[:], decay[:], pref[:], 0.0, ALU.mult, ALU.add))
                ve.wait_ge(s_qn, KC * b + c + 1)
                ve.tensor_tensor(yt[:], qt[:], kt[:], ALU.mult).then_inc(s_qm, 1)
                ve.wait_ge(s_qm, KC * b + c + 1)
                ve.wait_ge(s_ina, job + JOB_G + 1)
                own.do(ve.tensor_tensor(yt[:], yt[:], gt[:], ALU.mult))
                ve.wait_ge(s_w, KC * b + c + 1)
                ve.tensor_tensor(yt[:], yt[:], vt[:], ALU.add).then_inc(s_y, 1)

            def y_low(b, c):
                ve.wait_ge(s_yh, KC * b + c + 1)
                ve.tensor_tensor(y_lo[:, c, :], yt[:], y_hi[:, c, :], ALU.subtract).then_inc(s_yl, 1)

            def split_in(g):
                ve.wait_ge(s_whi, 3 + g)
                ve.tensor_tensor(win_lo[:, g].rearrange("p r k n -> p (r k n)"), raw[:, (g + 2) % 3, :],
                                 win_hi[:, g].rearrange("p r k n -> p (r k n)"), ALU.subtract).then_inc(s_wlo, 1)

            def attention(b, before):
                for c in range(KC):
                    group(b, c)
                    before(c)
                    y_low(b, c)

            ve.wait_ge(s_pc, 1)
            for n in range(NT):
                route_event(n)
            ve.wait_ge(s_rm, NT - 1)
            normalise(0, 0)
            ve.wait_ge(s_small, 16 * 6)
            choose(0)
            select(0, 0, 0)
            gate(0)
            select(0, 0, 1)
            split_hidden(0, 0, None)
            for c in range(KC):
                job = job_first(f"O{c}")
                if c < KC - 1:
                    split_hidden(0, c + 1, job)
                add_experts(0, c, job, bank_of(job))
            split_in(0)
            for t in range(NT):
                job = job_first(f"W{t}")
                w3_norm(0, t, job, bank_of(job))
            split_in(2)
            split_in(1)
            own.do(ve.memset(starts[:], 0.0))

            base = own.base + own.n
            with ve.Fori(0, B - 1) as b:
                own.base, own.n = base + b * VE_ROW_STEPS, 0

                def before(c):
                    if c == 0:
                        select(b + 1, b + 1, 0)
                        select(b + 1, b + 1, 1)
                    if c == 1:
                        normalise(b + 1, b + 1)

                attention(b, before)
                split_hidden(b + 1, 0, None)
                for name in ROW:
                    job, n = job_row(b, name), int(name[1])
                    bank = bank_of(row_base + ROW.index(name), name)
                    if name[0] == "O":
                        if n < KC - 1:
                            split_hidden(b + 1, n + 1, job)
                        add_experts(b + 1, n, job, bank)
                        if n == 1:
                            own.do(ve.tensor_copy(x1p[:, NT - 1, :], x1[:, NT - 1, :]))
                    elif name[0] == "W":
                        w3_norm(b + 1, n, job, bank)
                    elif n < NT - 1:
                        out_add(n, job, bank, x1, x1p)
                    else:
                        out_add(n, job, bank, x1p, x1p)
                assert own.n == VE_ROW_STEPS, own.n

            own.base, own.n = base + (B - 1) * VE_ROW_STEPS, 0

            def early(c):
                if c in (1, 2):
                    route_event(NT + c - 1)

            attention(B - 1, early)
            for t in range(NT):
                out_add(t, job_last(f"A{t}"), bank_of(job_last(f"A{t}"), f"last A{t}"), x1, x1)
                if t < 2:
                    ve.wait_ge(s_obf, job_last(f"A{t}") + 1)
                    route_event(NT + 2 + t)
            ve.wait_ge(s_obf, late_base)
            for n in range(NT + 4, len(EVENTS)):
                route_event(n)
            ve.wait_ge(s_rm, 2 * NT - 1)
            normalise(B, 0)
            choose(1)
            select(0, B, 0)
            gate(1)
            select(0, B, 1)
            hidden_lo(B, 0)
            hidden_lo(B, 1)
            normalise(B + 1, 1)
            for f in range(B, 2 * B):
                for c in range(KC):
                    if f > B:
                        job = job_late(f - 1, f"W{c}")
                        if f > B + 1:
                            ve.wait_ge(s_out[c], 16 * (f - B - 1))
                        elif c == 0:
                            ve.wait_ge(s_x2, 16 * NT * B)
                        w3_add(f - 1, c, job, bank_of(job))
                    job = job_late(f, f"O{c}")
                    add_experts(f, c, job, bank_of(job))
                    if f + 1 < 2 * B:
                        if c == 0 and f > B:
                            ve.wait_ge(s_t1, KC * (f + 1))
                            normalise(f + 1, f + 1 - B)
                        if c in (1, 2):
                            select(f + 1 - B, f + 1, c - 1)
                        if c == 3:
                            hidden_lo(f + 1, 0)
                            hidden_lo(f + 1, 1)
                    if c < 2:
                        hidden_lo(f, c + 2)
            for t in range(NT):
                job = job_late(2 * B - 1, f"W{t}")
                ve.wait_ge(s_out[t], 16 * (B - 1))
                w3_add(2 * B - 1, t, job, bank_of(job))


VE_ROW_STEPS = 54


def kernel(**inputs):
    import numpy as np
    import concourse.bacc as bacc
    from concourse.bass_utils import run_bass_kernel_spmd

    a = {k.replace("L0_attn_", "").replace("L0_ffn_", ""): np.asarray(v) for k, v in inputs.items()}
    w_in = a["w_in"].reshape(5, KC, P, KC, P)[[0, 3, 1, 2, 4]].transpose(1, 4, 0, 3, 2)
    arrays = {
        "x": a["x"],
        "w_in": w_in.reshape(KC, P, ROLES * KC * P),
        "w_out": a["w_out"].T.reshape(KC, P, D).transpose(1, 0, 2),
        "switch_w": a["switch_w"].reshape(E, NT, P, D // HD, HD).transpose(2, 1, 3, 0, 4),
        "switch_b": a["switch_b"],
        "w1": a["w1"].transpose(2, 1, 0),
        "b1": a["b1"].T,
        "w2": a["w2"].transpose(2, 1, 0),
        "b2": a["b2"].T,
        "w3": a["w3"].T.reshape(KC, P, D).transpose(1, 0, 2),
        "b3": a["b3"],
    }
    nc = bacc.Bacc("TRN2", target_bir_lowering=False, num_devices=1)
    feed, args = {}, []
    for name, arr in arrays.items():
        arr = np.ascontiguousarray(arr)
        feed[f"in_{name}"] = arr
        args.append(nc.dram_tensor(f"in_{name}", arr.shape, mybir.dt.from_np(arr.dtype), kind="ExternalInput").ap())
    args.append(nc.dram_tensor("out_0", (B, S, D), F32, kind="ExternalOutput").ap())
    macaron_kernel(nc, *args)
    r = run_bass_kernel_spmd(nc, [feed], core_ids=[0])
    return r.results[0]["out_0"]
```
